# Optimizing a Trainium2 kernel written in Bass

```python
import numpy as np
import jax
import jax.numpy as jnp

def _softmax(x, axis=-1):
    return jax.nn.softmax(x, axis=axis)

def _gelu(x):
    return jax.nn.gelu(x, approximate=True)

def _silu(x):
    return jax.nn.silu(x)

def _sigmoid(x):
    return jax.nn.sigmoid(x)

def _layernorm(x, axis=-1, eps=1e-05):
    m = jnp.mean(x, axis=axis, keepdims=True)
    v = jnp.var(x, axis=axis, keepdims=True)
    return (x - m) / jnp.sqrt(v + eps)

def _scatter_add(tgt, idx, src, axis=0):
    return tgt.at[idx].add(src)

def _segment_sum(src, seg, n):
    return jax.ops.segment_sum(src, seg, n)
kernel_name = 'mk_adj_resnorm_d4_adj_r2_4a8c3d'

def setup_inputs(seed: int=0):
    np.random.seed(seed)
    _w = jnp.asarray

    def _rec_inputs():
        import jax
        import jax.numpy as jnp
        _gk = jax.random.key(seed)
        x = -0.006082 + 1.001 * jax.random.normal(jax.random.fold_in(_gk, 1), (1354, 64), jnp.float32)
        _a = jax.random.bernoulli(jax.random.fold_in(_gk, 2), 0.00295421, (1354, 1354))
        _a = jnp.logical_or(_a, jnp.swapaxes(_a, -1, -2))
        _a = jnp.logical_or(_a, jnp.eye(1354, dtype=bool))
        adj = _a.astype(jnp.int32)
        return (x, adj)
    x, adj = _rec_inputs()

    def _L0_gnn_setup():
        import jax, jax.numpy as jnp
        import numpy as np
        NEG_SLOPE = 0.01
        key = jax.random.key(seed)
        ks = jax.random.split(key, 5)
        N, D_IN, D_OUT = (512, 64, 64)
        node_feats = jax.random.normal(ks[0], (N, D_IN), dtype=jnp.float32)
        fc_w = jax.random.normal(ks[1], (2 * D_IN, D_OUT), dtype=jnp.float32) * (1.0 / np.sqrt(2 * D_IN))
        fc_b = jnp.zeros((D_OUT,), dtype=jnp.float32)
        attn_w = jax.random.normal(ks[2], (D_OUT, 1), dtype=jnp.float32) * (1.0 / np.sqrt(D_OUT))
        attn_b = jnp.zeros((1,), dtype=jnp.float32)
        adj = jax.random.randint(ks[3], (N, N), 0, 2, dtype=jnp.int64)
        return {'node_feats': node_feats, 'fc_w': fc_w, 'fc_b': fc_b, 'attn_w': attn_w, 'attn_b': attn_b, 'adj': adj}
    _L0_gnn_all = _L0_gnn_setup()
    _L0_gnn_in = {k: v for k, v in _L0_gnn_all.items() if k in ('fc_w', 'fc_b', 'attn_w', 'attn_b')}
    del _L0_gnn_all

    def _L1_gnn_setup():
        import jax, jax.numpy as jnp
        import numpy as np
        N = 8192
        D = 64
        key = jax.random.key(seed)
        kx, ka = jax.random.split(key)
        x = jax.random.normal(kx, (N, D), dtype=jnp.float32)
        adj = jax.random.randint(ka, (N, N), 0, 2, dtype=jnp.int32)
        return {'x': x, 'adj': adj}
    _L1_gnn_all = _L1_gnn_setup()
    _L1_gnn_in = {k: v for k, v in _L1_gnn_all.items() if k in ()}
    del _L1_gnn_all

    def _L2_gnn_setup():
        import jax, jax.numpy as jnp
        import numpy as np
        N = 1024
        ATOM_D = 64
        H = 8
        NB = 8
        D = ATOM_D * H
        NEG_SLOPE = 0.2
        key = jax.random.key(seed)
        ks = jax.random.split(key, 12)
        inp = {'atom_embeddings': jax.random.normal(ks[0], (N, ATOM_D), dtype=jnp.float32), 'edges': jax.random.randint(ks[1], (N, N), -1, NB, dtype=jnp.int32), 'Qw': jax.random.normal(ks[2], (ATOM_D, D), dtype=jnp.float32) / np.sqrt(ATOM_D), 'Qb': jnp.zeros((D,), dtype=jnp.float32), 'Kw': jax.random.normal(ks[3], (ATOM_D, D), dtype=jnp.float32) / np.sqrt(ATOM_D), 'Kb': jnp.zeros((D,), dtype=jnp.float32), 'Vw': jax.random.normal(ks[4], (ATOM_D, D), dtype=jnp.float32) / np.sqrt(ATOM_D), 'Vb': jnp.zeros((D,), dtype=jnp.float32), 'a': jax.random.normal(ks[5], (NB, 2 * D, H), dtype=jnp.float32) * np.sqrt(2.0 / (2 * D + H)) * 1.414, 'Pw': jax.random.normal(ks[6], (D, ATOM_D), dtype=jnp.float32) / np.sqrt(D), 'Pb': jnp.zeros((ATOM_D,), dtype=jnp.float32)}
        return inp
    _L2_gnn_all = _L2_gnn_setup()
    _L2_gnn_in = {k: v for k, v in _L2_gnn_all.items() if k in ('Qw', 'Qb', 'Kw', 'Kb', 'Vw', 'Vb', 'a', 'Pw', 'Pb')}
    del _L2_gnn_all

    def _L3_gnn_setup():
        import jax, jax.numpy as jnp
        import numpy as np
        ALPHA = 0.2
        NEG_INF = -9000000000000000.0
        key = jax.random.key(seed)
        k1, k2, k3, k4 = jax.random.split(key, 4)
        N, F_IN, F_OUT = (512, 64, 64)
        h = jax.random.normal(k1, (N, F_IN), dtype=jnp.float32)
        adj = jax.random.randint(k2, (N, N), 0, 2, dtype=jnp.int32)
        lim_W = 1.414 * np.sqrt(6.0 / (F_IN + F_OUT))
        W = jax.random.uniform(k3, (F_IN, F_OUT), minval=-lim_W, maxval=lim_W, dtype=jnp.float32)
        lim_a = 1.414 * np.sqrt(6.0 / (2 * F_OUT + 1))
        a = jax.random.uniform(k4, (2 * F_OUT, 1), minval=-lim_a, maxval=lim_a, dtype=jnp.float32)
        return {'h': h, 'adj': adj, 'W': W, 'a': a}
    _L3_gnn_all = _L3_gnn_setup()
    _L3_gnn_in = {k: v for k, v in _L3_gnn_all.items() if k in ('W', 'a')}
    del _L3_gnn_all
    return {'x': x, 'adj': adj, 'L0_gnn_fc_w': _L0_gnn_in['fc_w'], 'L0_gnn_fc_b': _L0_gnn_in['fc_b'], 'L0_gnn_attn_w': _L0_gnn_in['attn_w'], 'L0_gnn_attn_b': _L0_gnn_in['attn_b'], 'L2_gnn_Qw': _L2_gnn_in['Qw'], 'L2_gnn_Qb': _L2_gnn_in['Qb'], 'L2_gnn_Kw': _L2_gnn_in['Kw'], 'L2_gnn_Kb': _L2_gnn_in['Kb'], 'L2_gnn_Vw': _L2_gnn_in['Vw'], 'L2_gnn_Vb': _L2_gnn_in['Vb'], 'L2_gnn_a': _L2_gnn_in['a'], 'L2_gnn_Pw': _L2_gnn_in['Pw'], 'L2_gnn_Pb': _L2_gnn_in['Pb'], 'L3_gnn_W': _L3_gnn_in['W'], 'L3_gnn_a': _L3_gnn_in['a']}

def reference(x, adj, L0_gnn_fc_w, L0_gnn_fc_b, L0_gnn_attn_w, L0_gnn_attn_b, L2_gnn_Qw, L2_gnn_Qb, L2_gnn_Kw, L2_gnn_Kb, L2_gnn_Vw, L2_gnn_Vb, L2_gnn_a, L2_gnn_Pw, L2_gnn_Pb, L3_gnn_W, L3_gnn_a):
    import jax
    import jax.numpy as jnp

    def _L0_gnn_ref(node_feats, fc_w, fc_b, attn_w, attn_b, adj):
        import jax, jax.numpy as jnp
        import numpy as np
        NEG_SLOPE = 0.01
        N = node_feats.shape[0]
        neigh = node_feats[adj]
        self_f = jnp.broadcast_to(node_feats[:, None, :], neigh.shape)
        h = jnp.concatenate([self_f, neigh], axis=-1)
        h = jax.nn.leaky_relu(h @ fc_w + fc_b, NEG_SLOPE)
        scores = (h @ attn_w)[..., 0] + attn_b[0]
        scores = jnp.where(adj != 0, scores, -jnp.inf)
        attn = jax.nn.softmax(scores, axis=1)
        return attn @ node_feats

    def _L1_gnn_ref(x, adj):
        import jax, jax.numpy as jnp
        import numpy as np
        N = 8192
        D = 64
        a = (adj == 1).astype(x.dtype)
        return jnp.matmul(a, x) + x

    def _L2_gnn_ref(atom_embeddings, edges, Qw, Qb, Kw, Kb, Vw, Vb, a, Pw, Pb):
        import jax, jax.numpy as jnp
        import numpy as np
        N = 1024
        ATOM_D = 64
        H = 8
        NB = 8
        D = ATOM_D * H
        NEG_SLOPE = 0.2
        n, d = atom_embeddings.shape
        nb, two_d, h = a.shape
        D_ = two_d // 2
        Q = atom_embeddings @ Qw + Qb
        K = atom_embeddings @ Kw + Kb
        V = atom_embeddings @ Vw + Vb
        A1 = a[:, :D_, :]
        A2 = a[:, D_:, :]
        S1 = jnp.einsum('id,kdh->ikh', Q, A1)
        S2 = jnp.einsum('jd,kdh->jkh', K, A2)
        kidx = jnp.clip(edges, 0, nb - 1)
        rows = jnp.arange(n)
        e = S1[rows[:, None], kidx] + S2[rows[None, :], kidx]
        valid = (edges >= 0)[..., None]
        e = jnp.where(valid, jax.nn.leaky_relu(e, negative_slope=NEG_SLOPE), 0.0)
        attn = jax.nn.softmax(e, axis=1)
        Vh = V.reshape(n, h, d)
        out = jnp.einsum('ijh,jhd->ihd', attn, Vh).reshape(n, h * d)
        return out @ Pw + Pb

    def _L3_gnn_ref(h, adj, W, a):
        import jax, jax.numpy as jnp
        import numpy as np
        ALPHA = 0.2
        NEG_INF = -9000000000000000.0
        F_OUT = W.shape[1]
        Wh = h @ W
        a1, a2 = (a[:F_OUT, 0], a[F_OUT:, 0])
        e = (Wh @ a1)[:, None] + (Wh @ a2)[None, :]
        e = jax.nn.leaky_relu(e, negative_slope=ALPHA)
        scores = jnp.where(adj > 0, e, jnp.float32(NEG_INF))
        attention = jax.nn.softmax(scores, axis=1)
        h_prime = attention @ Wh
        return jax.nn.elu(h_prime)
    x = _layernorm(x + _L0_gnn_ref(x, L0_gnn_fc_w, L0_gnn_fc_b, L0_gnn_attn_w, L0_gnn_attn_b, adj), axis=-1)
    x = _layernorm(x + _L1_gnn_ref(x, adj), axis=-1)
    x = _layernorm(x + _L2_gnn_ref(x, adj, L2_gnn_Qw, L2_gnn_Qb, L2_gnn_Kw, L2_gnn_Kb, L2_gnn_Vw, L2_gnn_Vb, L2_gnn_a, L2_gnn_Pw, L2_gnn_Pb), axis=-1)
    x = _layernorm(x + _L3_gnn_ref(x, adj, L3_gnn_W, L3_gnn_a), axis=-1)
    return x

_drawn_inputs = setup_inputs


def setup_inputs(seed=0):
    import zlib

    import numpy as np

    out = dict(_drawn_inputs(seed))
    spreads = {'L0_gnn_fc_b': (0.0, 0.1),
     'L2_gnn_Qb': (0.0, 0.8),
     'L2_gnn_Kb': (0.0, 0.8),
     'L2_gnn_Vb': (0.0, 0.1),
     'L2_gnn_Pb': (0.0, 0.1)}
    factors = {}
    for name, (base, spread) in spreads.items():
        noise = np.random.default_rng([zlib.crc32(name.encode()), seed]).standard_normal(out[name].shape)
        drawn = base * np.exp(spread * noise) if base else spread * noise
        out[name] = jnp.asarray(drawn.astype(out[name].dtype))
    for name, factor in factors.items():
        out[name] = (out[name] * factor).astype(out[name].dtype)
    return out
```

```python
from contextlib import ExitStack

import numpy as np
import concourse.bass as bass
from concourse import mybir
from concourse.alu_op_type import AluOpType as ALU

ACT = mybir.ActivationFunctionType
F32 = mybir.dt.float32
BF16 = mybir.dt.bfloat16
I32 = mybir.dt.int32
U16 = mybir.dt.uint16
X_AXIS = mybir.AxisListType.X

P = 128
N, D = 1354, 64
T = -(-N // P)
NP = T * P
LAST = N - (T - 1) * P
H = 8
DH = H * D
EPS = 1e-5
CHUNKS = [(c, min(512, N - c)) for c in range(0, N, 512)]
PADDED = [(c, min(512, NP - c)) for c in range(0, NP, 512)]
HALF = N // 2
GROUPS = [(0, 4), (4, 8), (8, T)]
W0 = 3 * D + 1
W2 = D + 1
W3 = D + 2
STAGES = 5
TA = 7


def rows_of(t):
    return LAST if t == T - 1 else P


def graph_kernel(nc, x, adj, fc_w, fc_b, attn_w, attn_b, Qw, Qb, Kw, Kb, Vw, Vb, a, Pw, Pb, W, a3, out):
    with ExitStack() as ctx:
        def sb(name, shape, dt=F32):
            return ctx.enter_context(nc.sbuf_tensor(name, shape, dt))

        def sem(name):
            return ctx.enter_context(nc.semaphore(name))

        AT = sb("AT", [P, T, NP], BF16)
        Z = sb("Z", [P, T, N])
        Zflat = Z[:, :, :].rearrange("p t n -> p (t n)")
        AN_WORDS = T * NP // 2
        AN = Zflat[:, 0:AN_WORDS].bitcast(BF16).rearrange("p (t n) -> p t n", t=T)
        STAGE = Zflat[:, AN_WORDS:AN_WORDS + STAGES * N].bitcast(I32).rearrange("p (s n) -> p s n", s=STAGES)
        X = [sb(f"X{i}", [P, T, D]) for i in range(4)]
        XS = [sb(f"XS{i}", [P, T, W0], BF16) for i in range(2)]
        RES = sb("RES", [P, T, D])
        Y = sb("Y", [P, T, D])
        CEN = sb("CEN", [P, T, D])
        SQ = sb("SQ", [P, T, D])
        STAT = sb("STAT", [P, 8, T])
        XT = sb("XT", [W2, NP])
        NUMT = sb("NUMT", [W2, NP])
        LHS1 = sb("LHS1", [P, H, NP], BF16)
        RHS1 = sb("RHS1", [P, H, N], BF16)
        ROW0 = [sb(f"ROW0_{i}", [P, N]) for i in range(2)]
        VST = [sb(f"VST{i}", [P, T, W2]) for i in range(2)]
        B0 = sb("B0", [P, T, H])
        NEGC = sb("NEGC", [P, H])
        AB = Z[0:4 * H, T - 1, :]
        R1 = Z[0:4 * H, T - 2, :]
        THIRD = [Z[0:4 * H, T - 5 + i, :].bitcast(BF16)[:, 0:N] for i in range(3)]
        WH = sb("WH", [P, T, W3])
        HS = NUMT[0:D, :]
        XT_TMP = LHS1[0:D, 0:2, :].rearrange("p h n -> p (h n)").bitcast(F32)
        IDF = sb("IDF", [P, P])
        IDB = sb("IDB", [P, P], BF16)
        SEL = sb("SEL", [P, P], BF16)
        ONES = sb("ONES", [P, P])
        QS, KS = ROW0[0][0:W2, 0:DH], ROW0[0][0:W2, DH:2 * DH]
        VS = ROW0[1][0:W2, 0:DH]
        QKT = ROW0[1][:, DH:DH + 8 * W2].rearrange("p (c d) -> p c d", d=W2)
        VWT = VST[0][0:D, 0:H, :]
        PWS = VST[1][0:D, 0:H, 0:D]
        AW = sb("AW", [P, 8, 2, H])
        W32 = sb("W32", [W2, 4 * H])
        VP = sb("VP", [W2, H, W2])
        W3S = sb("W3S", [W2, W3])
        A3 = sb("A3", [D, 2])
        WT = sb("WT", [D, D])
        WA3 = sb("WA3", [D, 2])
        FREP = sb("FREP", [D, P])
        GREP = sb("GREP", [D, P])
        FC1 = sb("FC1", [D, D])
        FC2 = sb("FC2", [D, D])
        FCB = sb("FCB", [D, 1])
        HB = sb("HB", [D, 1])
        ATW = sb("ATW", [D, 1])
        ATB = sb("ATB", [P, 1])
        PBB = sb("PBB", [P, D])
        SC = sb("SC", [P, 3, T])
        WROW = sb("WROW", [P, T])
        MX = sb("MX", [4 * H, 1])
        MXR = sb("MXR", [4 * H, P])
        G2 = sb("G2", [P, 3, 2 * H])
        RDEN = sb("RDEN", [P, T])
        NRM = sb("NRM", [P, T, D])
        C3 = sb("C3", [P, 4])

        PS = ctx.enter_context(nc.psum_tensor("PS", [P, 8, 512], F32))
        PSflat = PS[:, :, :].rearrange("p b n -> p (b n)")
        PSN = PSflat[:, 0:3072].rearrange("p (t n) -> p t n", n=256)
        PSTR = PSflat[:, 3072:4096].bitcast(BF16)
        ACC = PSflat[:, 0:N]
        ZP = PSflat[:, 1536:1536 + N]
        MISC = PSflat[:, 3072:4096]

        def two_banks(width):
            return (PS[:, 6, 0:TA * width].rearrange("p (t n) -> p t n", n=width),
                    PS[:, 7, 0:(T - TA) * width].rearrange("p (t n) -> p t n", n=width),
                    lambda t: PS[:, 6 + t // TA, t % TA * width:t % TA * width + width])

        VA, VB, v_block = two_banks(W2)
        WHA, WHB, wh_block = two_banks(W3)

        x_in, w_in, wb_in = sem("x_in"), sem("w_in"), sem("wb_in")
        adj_in = [sem(f"adj_in{t}") for t in range(T)]
        w3_zero = sem("w3_zero")
        consts, x_pad, idents, an_pads, ops_ones = sem("consts"), sem("x_pad"), sem("idents"), sem("an_pads"), sem("ops_ones")
        x0t_mm, x0t_sb, wts_mm, wts_sb = sem("x0t_mm"), sem("x0t_sb"), sem("wts_mm"), sem("wts_sb")
        fold_mm, fold_sb, hid_mm, hid_sb = sem("fold_mm"), sem("fold_sb"), sem("hid_mm"), sem("hid_sb")
        score_mm, score_dif, score_exp = sem("score_mm"), sem("score_dif"), sem("score_exp")
        xs_ready, an_ready, at_mm, at_lo, at_hi = sem("xs_ready"), sem("an_ready"), sem("at_mm"), sem("at_lo"), sem("at_hi")
        sum0_mm, sum1_mm = sem("sum0_mm"), sem("sum1_mm")
        var_ready, rstd_ready, x_ready = sem("var_ready"), sem("rstd_ready"), sem("x_ready")
        xt_mm, xt_sb = sem("xt_mm"), sem("xt_sb")
        ab_mm, ab_sb, third_ready, third_in = sem("ab_mm"), sem("ab_sb"), sem("third_ready"), sem("third_in")
        b0_mm, mxr_ready, max_mm, guards = sem("b0_mm"), sem("mxr_ready"), sem("max_mm"), sem("guards")
        row_mm, row_sb, val_mm, val_sb = sem("row_mm"), sem("row_sb"), sem("val_mm"), sem("val_sb")
        tiles_picked = sem("tiles_picked")
        z0_ready, z1_mm, z_ready = sem("z0_ready"), sem("z1_mm"), sem("z_ready")
        leaky_ready, p_ready, p_used = sem("leaky_ready"), sem("p_ready"), sem("p_used")
        acc_mm, acc_sb, num_mm, num_added, norm_step = sem("acc_mm"), sem("acc_sb"), sem("num_mm"), sem("num_added"), sem("norm_step")
        fg_mm, wh_mm, wh_sb, guard3 = sem("fg_mm"), sem("wh_mm"), sem("wh_sb"), sem("guard3")
        z3_ready, waits_done = sem("z3_ready"), sem("waits_done")
        leaky3, p3_exp, p3_ready, acc3_mm, acc3_sb, num3_mm = sem("leaky3"), sem("p3_exp"), sem("p3_ready"), sem("acc3_mm"), sem("acc3_sb"), sem("num3_mm")
        elu_in, elu_exp, out_done, dve_done = sem("elu_in"), sem("elu_exp"), sem("out_done"), sem("dve_done")

        block = ctx.enter_context(nc.Block())

        @block.sync
        def _(sp):
            sp.wait_ge(x_pad, 1)
            sp.dma_start(X[0][:, 0:T - 1, :], x[0:(T - 1) * P, :].rearrange("(t p) d -> p t d", p=P)).then_inc(x_in, 16)
            sp.dma_start(X[0][0:LAST, T - 1, :], x[(T - 1) * P:N, :]).then_inc(x_in, 16)
            for t in range(T):
                if t >= STAGES:
                    sp.wait_ge(an_ready, t - STAGES + 1)
                sp.dma_start(STAGE[0:rows_of(t), t % STAGES, :], adj[t * P:t * P + rows_of(t), :]).then_inc(adj_in[t], 16)
            sp.wait_ge(ops_ones, 4)
            for s in range(3):
                sp.wait_ge(third_ready, s + 1)
                sp.dma_start(RHS1[s:s + 1, :, :], THIRD[s][0:H, :]).then_inc(third_in, 16)
                sp.dma_start(RHS1[3 + s:4 + s, :, :], THIRD[s][H:2 * H, :]).then_inc(third_in, 16)
                sp.dma_start(LHS1[6 + s:7 + s, :, 0:N], THIRD[s][3 * H:4 * H, :]).then_inc(third_in, 16)
            sp.wait_ge(x_ready, 3 * len(GROUPS) + 1)
            sp.dma_start(out[0:(T - 1) * P, :].rearrange("(t p) d -> p t d", p=P), Y[:, 0:T - 1, :]).then_inc(out_done, 16)
            sp.dma_start(out[(T - 1) * P:N, :], Y[0:LAST, T - 1, :]).then_inc(out_done, 16)
            sp.wait_ge(out_done, 32)

        @block.gpsimd
        def _(pool):
            count = {}

            def alone(ins, signal):
                count[signal.name] = count.get(signal.name, 0) + 1
                ins.then_inc(signal, 1)
                pool.wait_ge(signal, count[signal.name])

            alone(nc.gpsimd.memset(X[0][:, T - 1, :], 0.0), x_pad)
            alone(nc.gpsimd.memset(ONES[:, :], 1.0), idents)
            alone(nc.gpsimd.affine_select(out=IDF[:, :], in_=ONES[:, :], compare_op=ALU.is_equal, fill=0.0, base=0,
                                          pattern=[[-1, P]], channel_multiplier=1), idents)
            alone(nc.gpsimd.tensor_copy(IDB[:, :], IDF[:, :]), idents)
            for dst, weight, bias in ((QS, Qw, Qb), (KS, Kw, Kb), (VS, Vw, Vb)):
                pool.dma_start(dst[0:D, :], weight).then_inc(w_in, 16)
                pool.dma_start(dst[D:W2, :], bias.unsqueeze(0)).then_inc(w_in, 16)
            pool.dma_start(PWS[:, :, :], Pw.rearrange("(h d) o -> d h o", d=D)).then_inc(w_in, 16)
            alone(nc.gpsimd.memset(W3S[:, :], 0.0), w3_zero)
            alone(nc.gpsimd.memset(W3S[D:W2, D:D + 1], 1.0), consts)
            alone(nc.gpsimd.memset(XT[D:W2, :], 1.0), consts)
            alone(nc.gpsimd.memset(XS[0][:, :, W0 - 1:W0], 1.0), consts)
            alone(nc.gpsimd.memset(AN[:, :, N:NP], 0.0), an_pads)
            alone(nc.gpsimd.memset(AN[:, T - 1, 0:N], 1.0), an_pads)
            alone(nc.gpsimd.memset(VP[:, :, D:W2], 0.0), consts)
            alone(nc.gpsimd.memset(VP[D:W2, :, D:W2], 1.0), consts)
            alone(nc.gpsimd.memset(SEL[:, :], 0.0), consts)
            alone(nc.gpsimd.memset(SEL[0:3, :], 1.0), consts)
            pool.wait_ge(hid_sb, 1)
            alone(nc.gpsimd.memset(RHS1[:, :, :], 1.0), ops_ones)
            alone(nc.gpsimd.memset(LHS1[:, :, :], 0.0), ops_ones)
            alone(nc.gpsimd.memset(LHS1[0:9, :, :], 1.0), ops_ones)
            alone(nc.gpsimd.memset(LHS1[0:3, :, :], 0.0), ops_ones)
            for n in range(3 * len(GROUPS) + 1):
                g = GROUPS[n % len(GROUPS)] if n < 3 * len(GROUPS) else (0, T)
                pool.wait_ge(var_ready, n + 1)
                alone(nc.gpsimd.tensor_tensor(STAT[:, 3, g[0]:g[1]], STAT[:, 2, g[0]:g[1]], STAT[:, 7, g[0]:g[1]],
                                              ALU.pow), rstd_ready)

        @block.scalar
        def _(act):
            act.dma_start(FC1[:, :], fc_w[0:D, :]).then_inc(wb_in, 16)
            act.dma_start(FC2[:, :], fc_w[D:2 * D, :]).then_inc(wb_in, 16)
            act.dma_start(FCB[:, :], fc_b.rearrange("(d o) -> d o", o=1)).then_inc(wb_in, 16)
            act.dma_start(ATW[:, :], attn_w).then_inc(wb_in, 16)
            act.dma_start(ATB[:, :], attn_b.partition_broadcast(P)).then_inc(wb_in, 16)
            act.dma_start(PBB[:, :], Pb.partition_broadcast(P)).then_inc(wb_in, 16)
            act.dma_start(A3[:, 0:1], a3[0:D, :]).then_inc(wb_in, 16)
            act.dma_start(A3[:, 1:2], a3[D:2 * D, :]).then_inc(wb_in, 16)
            for k in range(2):
                act.dma_start(AW[:, :, k, :], a[k].rearrange("(c p) h -> p c h", p=P)).then_inc(wb_in, 16)
            act.wait_ge(w3_zero, 1)
            act.dma_start(W3S[0:D, 0:D], W).then_inc(wb_in, 16)

            act.wait_ge(x0t_mm, 1)
            nc.scalar.activation(XT[0:D, :], PSflat[0:D, 0:NP], ACT.Copy).then_inc(x0t_sb, 1)
            act.wait_ge(score_dif, 1)
            nc.scalar.activation(WROW[:, :], SC[:, 2, :], ACT.Exp).then_inc(score_exp, 1)

            act.wait_ge(an_pads, 2)
            for t in range(T):
                act.wait_ge(adj_in[t], 16)
                nc.scalar.activation(AN[0:rows_of(t), t, 0:N], STAGE[0:rows_of(t), t % STAGES, :], ACT.Copy).then_inc(an_ready, 1)
                if t >= 1:
                    act.wait_ge(at_mm, t)
                    nc.scalar.activation(AT[:, 8:T, (t - 1) * P:t * P], PSTR[:, 8 * P:T * P].rearrange("p (j i) -> p j i", i=P), ACT.Copy).then_inc(at_hi, 1)
            act.wait_ge(at_mm, T)
            nc.scalar.activation(AT[:, 8:T, (T - 1) * P:NP], PSTR[:, 8 * P:T * P].rearrange("p (j i) -> p j i", i=P), ACT.Copy).then_inc(at_hi, 1)

            def xt_copy(first):
                for n, (lo, hi) in enumerate(GROUPS):
                    act.wait_ge(xt_mm, first + n + 1)
                    nc.scalar.activation(XT[0:D, lo * P:hi * P], PS[0:D, 6 + n % 2, 0:(hi - lo) * P], ACT.Copy).then_inc(xt_sb, 1)

            xt_copy(0)
            for n, (c, w) in enumerate(CHUNKS):
                act.wait_ge(ab_mm, n + 1)
                nc.scalar.activation(AB[:, c:c + w], PSflat[0:4 * H, c:c + w], ACT.Copy).then_inc(ab_sb, 1)

            def row_copy(h, half, par):
                act.wait_ge(row_mm, 2 * h + half + 1)
                nc.scalar.activation(ROW0[par][:, half * HALF:(half + 1) * HALF], MISC[:, 0:HALF], ACT.Copy).then_inc(row_sb, 1)

            def val_copy(h, par):
                act.wait_ge(val_mm, h + 1)
                nc.scalar.activation(VST[par][:, 0:TA, :], VA, ACT.Copy)
                nc.scalar.activation(VST[par][:, TA:T, :], VB, ACT.Copy).then_inc(val_sb, 1)

            def z0(h, t, par, reused):
                if t == 0:
                    act.wait_ge(row_sb, 2 * h + 2)
                if reused:
                    act.wait_ge(p_used, (h - 1) * T + t + 1)
                act.sem_inc(waits_done, 1)
                nc.scalar.activation(Z[:, t, :], ROW0[par][:, :], ACT.Identity, bias=B0[:, t, bass.ds(h, 1)]).then_inc(z0_ready, 1)

            def exp(h, t):
                act.wait_ge(leaky_ready, h * T + t + 1)
                act.sem_inc(waits_done, 1)
                nc.scalar.activation(Z[:, t, :], Z[:, t, :], ACT.Exp, bias=NEGC[:, bass.ds(h, 1)]).then_inc(p_ready, 1)

            def sums_copy(h):
                for n, (c, w) in enumerate(CHUNKS):
                    act.wait_ge(acc_mm, 3 * h + n + 1)
                    nc.scalar.activation(NUMT[:, c:c + w], ACC[0:W2, c:c + w], ACT.Copy).then_inc(acc_sb, 1)

            def head(h, par, first, last):
                for t in range(T):
                    if t == 3 and not first:
                        sums_copy(h - 1)
                    if t < T - 1:
                        z0(h, t + 1, par, not first)
                    elif not last:
                        z0(h + 1, 0, 1 - par, True)
                    if t >= 2:
                        exp(h, t - 2)
                    elif not first:
                        exp(h - 1, T - 2 + t)
                    if not last:
                        if t in (7, 8):
                            row_copy(h + 1, t - 7, 1 - par)
                        if t == 9:
                            val_copy(h + 1, 1 - par)

            row_copy(0, 0, 0)
            row_copy(0, 1, 0)
            act.wait_ge(guards, 1)
            z0(0, 0, 0, False)
            val_copy(0, 0)
            head(0, 0, True, False)
            with act.Fori(0, H // 2 - 1) as pair:
                head(2 * pair + 1, 1, False, False)
                head(2 * pair + 2, 0, False, False)
            head(H - 1, 1, False, True)
            exp(H - 1, T - 2)
            exp(H - 1, T - 1)
            sums_copy(H - 1)

            xt_copy(len(GROUPS))
            act.wait_ge(wh_mm, 1)
            nc.scalar.activation(WH[:, 0:TA, :], WHA, ACT.Copy)
            nc.scalar.activation(WH[:, TA:T, :], WHB, ACT.Copy).then_inc(wh_sb, 1)
            act.wait_ge(wh_sb, 1)
            act.wait_ge(fg_mm, 1)
            act.wait_ge(p_used, H * T)
            act.wait_ge(guard3, 1)
            for t in range(T + 2):
                if t < T:
                    nc.scalar.activation(Z[:, t, :], ACC, ACT.Identity, bias=WH[:, t, D + 1:D + 2]).then_inc(z3_ready, 1)
                if t >= 2:
                    act.wait_ge(leaky3, t - 1)
                    nc.scalar.activation(Z[:, t - 2, :], Z[:, t - 2, :], ACT.Exp, bias=C3[:, 3:4]).then_inc(p3_exp, 1)
            for n, (c, w) in enumerate(CHUNKS):
                act.wait_ge(acc3_mm, n + 1)
                nc.scalar.activation(NUMT[:, c:c + w], ZP[0:W2, c:c + w], ACT.Copy).then_inc(acc3_sb, 1)
            act.wait_ge(elu_in, 1)
            nc.scalar.activation(SQ[:, :, :], CEN[:, :, :], ACT.Exp).then_inc(elu_exp, 1)

        @block.vector
        def _(dve):
            done = [0]
            chain = sem("dve_chain")

            def link(ins):
                done[0] += 1
                ins.then_inc(chain, 1)
                dve.wait_ge(chain, done[0])

            def wide(ap, n):
                return ap.unsqueeze(2).to_broadcast([P, n, D])

            def thirds(src, dst, lo, hi):
                link(nc.vector.tensor_copy(dst[:, lo:hi, 0:D], src[:, lo:hi, :]))
                link(nc.vector.tensor_tensor(RES[:, lo:hi, :], src[:, lo:hi, :], dst[:, lo:hi, 0:D], ALU.subtract))
                link(nc.vector.tensor_copy(dst[:, lo:hi, D:2 * D], RES[:, lo:hi, :]))
                return nc.vector.tensor_tensor(dst[:, lo:hi, 2 * D:3 * D], RES[:, lo:hi, :], dst[:, lo:hi, D:2 * D], ALU.subtract)

            norms = [0]

            def layer_norm(src, dst, lo, hi):
                n = hi - lo
                link(nc.vector.tensor_reduce(STAT[:, 0, lo:hi], src[:, lo:hi, :], X_AXIS, ALU.add))
                link(nc.vector.tensor_scalar(STAT[:, 1, lo:hi], STAT[:, 0, lo:hi], 1.0 / D, None, ALU.mult))
                link(nc.vector.tensor_tensor(CEN[:, lo:hi, :], src[:, lo:hi, :], wide(STAT[:, 1, lo:hi], n), ALU.subtract))
                link(nc.vector.tensor_tensor(SQ[:, lo:hi, :], CEN[:, lo:hi, :], CEN[:, lo:hi, :], ALU.mult))
                link(nc.vector.tensor_reduce(STAT[:, 4, lo:hi], SQ[:, lo:hi, :], X_AXIS, ALU.add))
                nc.vector.tensor_scalar(STAT[:, 2, lo:hi], STAT[:, 4, lo:hi], 1.0 / D, EPS, ALU.mult, ALU.add).then_inc(var_ready, 1)
                norms[0] += 1
                dve.wait_ge(rstd_ready, norms[0])
                return nc.vector.tensor_tensor(dst[:, lo:hi, :], CEN[:, lo:hi, :], wide(STAT[:, 3, lo:hi], n), ALU.mult)

            def sum_thirds(dst, lo, hi):
                link(nc.vector.tensor_reduce(dst[:, lo:hi, :], PSN[:, lo:hi, 0:3 * D].rearrange("p t (s d) -> p t d s", s=3), X_AXIS, ALU.add))

            link(nc.vector.memset(STAT[:, 7, :], -0.5))
            link(nc.vector.memset(NUMT[:, :], 1.0))

            dve.wait_ge(x_in, 32)
            thirds(X[0], XS[0], 0, T).then_inc(xs_ready, 1)
            dve.wait_ge(wts_mm, 1)
            for half in range(2):
                nc.vector.tensor_copy(QKT[:, 4 * half:4 * half + 4, :], PS[:, 3 + half, 0:4 * W2].rearrange("p (c d) -> p c d", d=W2))
                nc.vector.tensor_copy(VWT[:, 4 * half:4 * half + 4, :], PS[0:D, 6 + half, 0:4 * W2].rearrange("p (h d) -> p h d", d=W2)).then_inc(wts_sb, 1)
            nc.vector.tensor_copy(WT[:, :], PS[0:D, 5, 0:D]).then_inc(wts_sb, 1)
            dve.wait_ge(hid_mm, 1)
            link(nc.vector.tensor_tensor(HB[:, :], PS[0:D, 5, 100:101], FCB[:, :], ALU.add))
            link(nc.vector.tensor_scalar(XT_TMP, PSflat[0:D, 0:NP], HB[:, 0:1], None, ALU.add))
            nc.vector.scalar_tensor_tensor(HS, XT_TMP, 0.01, XT_TMP, ALU.mult, ALU.max).then_inc(hid_sb, 1)
            dve.wait_ge(fold_mm, 1)
            nc.vector.tensor_copy(W32[:, :], PS[0:W2, 6, 0:4 * H])
            nc.vector.tensor_copy(VP[:, :, 0:D], PS[0:W2, 7, :].rearrange("p (h d) -> p h d", d=D))
            nc.vector.tensor_copy(W3S[0:D, D + 1:D + 2], PS[0:D, 3, 1:2])
            link(nc.vector.tensor_copy(WA3[:, :], PS[0:D, 3, 0:2]))
            nc.vector.tensor_scalar(FREP[:, :], ONES[0:D, :], WA3[:, 0:1], None, ALU.mult)
            nc.vector.tensor_scalar(GREP[:, :], ONES[0:D, :], WA3[:, 1:2], None, ALU.mult).then_inc(fold_sb, 1)
            dve.wait_ge(score_mm, 1)
            link(nc.vector.tensor_scalar(SC[:, 0, :], PS[:, 5, 128:128 + T], ATB[:, 0:1], None, ALU.add))
            link(nc.vector.tensor_tensor(SC[:, 1, :], SC[:, 0, :], SC[:, 0, :], ALU.max))
            nc.vector.tensor_tensor(SC[:, 2, :], SC[:, 0, :], SC[:, 1, :], ALU.subtract).then_inc(score_dif, 1)

            def layer0(lo, hi):
                n = hi - lo
                dve.wait_ge(sum0_mm, hi)
                sum_thirds(NRM, lo, hi)
                link(nc.vector.tensor_tensor(RDEN[:, lo:hi], PSN[:, lo:hi, W0 - 1], WROW[:, lo:hi], ALU.mult))
                link(nc.vector.reciprocal(STAT[:, 5, lo:hi], RDEN[:, lo:hi]))
                link(nc.vector.tensor_tensor(STAT[:, 6, lo:hi], STAT[:, 5, lo:hi], WROW[:, lo:hi], ALU.mult))
                link(nc.vector.tensor_tensor(NRM[:, lo:hi, :], NRM[:, lo:hi, :], wide(STAT[:, 6, lo:hi], n), ALU.mult))
                link(nc.vector.tensor_tensor(Y[:, lo:hi, :], NRM[:, lo:hi, :], X[0][:, lo:hi, :], ALU.add))
                link(layer_norm(Y, X[1], lo, hi))
                thirds(X[1], XS[1], lo, hi).then_inc(x_ready, 1)

            dve.wait_ge(score_exp, 1)
            for t in range(T):
                dve.wait_ge(at_mm, t + 1)
                nc.vector.tensor_copy(AT[:, 0:8, t * P:(t + 1) * P], PSTR[:, 0:8 * P].rearrange("p (j i) -> p j i", i=P)).then_inc(at_lo, 1)
                for lo, hi in GROUPS[:-1]:
                    if t == hi:
                        layer0(lo, hi)
            layer0(*GROUPS[-1])

            for lo, hi in GROUPS:
                dve.wait_ge(sum1_mm, hi)
                sum_thirds(NRM, lo, hi)
                link(nc.vector.tensor_tensor(NRM[:, lo:hi, :], NRM[:, lo:hi, :], X[1][:, lo:hi, :], ALU.add))
                link(nc.vector.tensor_tensor(Y[:, lo:hi, :], NRM[:, lo:hi, :], X[1][:, lo:hi, :], ALU.add))
                layer_norm(Y, X[2], lo, hi).then_inc(x_ready, 1)

            dve.wait_ge(at_hi, T)
            dve.wait_ge(ab_sb, len(CHUNKS))
            nc.vector.tensor_copy(THIRD[0][:, :], AB[:, :]).then_inc(third_ready, 1)
            dve.wait_ge(third_ready, 1)
            link(nc.vector.tensor_tensor(R1[:, :], AB[:, :], THIRD[0][:, :], ALU.subtract))
            nc.vector.tensor_copy(THIRD[1][:, :], R1[:, :]).then_inc(third_ready, 1)
            dve.wait_ge(third_ready, 2)
            nc.vector.tensor_tensor(THIRD[2][:, :], R1[:, :], THIRD[1][:, :], ALU.subtract).then_inc(third_ready, 1)
            link(nc.vector.tensor_reduce(MX[:, :], AB[:, :], X_AXIS, ALU.max))
            nc.vector.tensor_scalar(MXR[:, :], ONES[0:4 * H, :], MX[:, 0:1], None, ALU.mult).then_inc(mxr_ready, 1)
            dve.wait_ge(b0_mm, 1)
            link(nc.vector.tensor_copy(B0[:, :, :], PS[:, 3, 64:64 + T * H].rearrange("p (t h) -> p t h", h=H)))
            dve.wait_ge(max_mm, 1)
            link(nc.vector.tensor_copy(G2[:, 0, :], PS[:, 4, 0:2 * H]))
            link(nc.vector.tensor_tensor(G2[:, 1, :], PS[:, 4, 2 * H:4 * H], G2[:, 0, :], ALU.add))
            link(nc.vector.scalar_tensor_tensor(G2[:, 2, :], G2[:, 1, :], 0.2, G2[:, 1, :], ALU.mult, ALU.max))
            link(nc.vector.tensor_tensor(G2[:, 0, 0:H], G2[:, 2, 0:H], G2[:, 2, H:2 * H], ALU.max))
            nc.vector.tensor_scalar(NEGC[:, :], G2[:, 0, 0:H], -1.0, None, ALU.mult).then_inc(guards, 1)
            link(nc.vector.tensor_tensor(Y[:, :, :], X[2][:, :, :], PBB[:, :].unsqueeze(1).to_broadcast([P, T, D]), ALU.add))

            def pick(h, t):
                dve.wait_ge(z0_ready, h * T + t + 1)
                dve.wait_ge(z1_mm, h * T + t + 1)
                dve.sem_inc(tiles_picked, 1)
                nc.vector.copy_predicated(Z[:, t, :], AT[:, t, 0:N].bitcast(U16), ZP).then_inc(z_ready, 1)

            def leaky(h, t):
                dve.wait_ge(z_ready, h * T + t + 1)
                nc.vector.scalar_tensor_tensor(Z[:, t, :], Z[:, t, :], 0.2, Z[:, t, :], ALU.mult, ALU.max).then_inc(leaky_ready, 1)

            def add_head(h):
                dve.wait_ge(num_mm, h + 1)
                nc.vector.reciprocal(RDEN[:, 0:TA], VA[:, :, D])
                nc.vector.reciprocal(RDEN[:, TA:T], VB[:, :, D]).then_inc(norm_step, 1)
                dve.wait_ge(norm_step, 2 * h + 1)
                nc.vector.tensor_tensor(NRM[:, 0:TA, :], VA[:, :, 0:D], wide(RDEN[:, 0:TA], TA), ALU.mult)
                nc.vector.tensor_tensor(NRM[:, TA:T, :], VB[:, :, 0:D], wide(RDEN[:, TA:T], T - TA), ALU.mult).then_inc(norm_step, 1)
                dve.wait_ge(norm_step, 2 * h + 2)
                nc.vector.tensor_tensor(Y[:, :, :], Y[:, :, :], NRM[:, :, :], ALU.add).then_inc(num_added, 1)

            def head(h, first):
                for t in range(T):
                    pick(h, t)
                    if t > 0:
                        leaky(h, t - 1)
                    elif not first:
                        leaky(h - 1, T - 1)
                    if t == 5 and not first:
                        add_head(h - 1)

            head(0, True)
            with dve.Fori(1, H) as h:
                head(h, False)
            leaky(H - 1, T - 1)
            add_head(H - 1)
            dve.wait_ge(num_added, H)
            for lo, hi in GROUPS:
                layer_norm(Y, X[3], lo, hi).then_inc(x_ready, 1)

            dve.wait_ge(fg_mm, 1)
            nc.vector.tensor_reduce(C3[:, 0:1], ACC, X_AXIS, ALU.max)
            dve.wait_ge(fg_mm, 2)
            link(nc.vector.tensor_reduce(C3[:, 1:2], ZP, X_AXIS, ALU.max))
            link(nc.vector.tensor_tensor(C3[:, 2:3], C3[:, 0:1], C3[:, 1:2], ALU.add))
            link(nc.vector.scalar_tensor_tensor(C3[:, 0:1], C3[:, 2:3], 0.2, C3[:, 2:3], ALU.mult, ALU.max))
            nc.vector.tensor_scalar(C3[:, 3:4], C3[:, 0:1], -1.0, None, ALU.mult).then_inc(guard3, 1)
            for t in range(T + 3):
                if t < T:
                    dve.wait_ge(z3_ready, t + 1)
                    nc.vector.scalar_tensor_tensor(Z[:, t, :], Z[:, t, :], 0.2, Z[:, t, :], ALU.mult, ALU.max).then_inc(leaky3, 1)
                if t >= 3:
                    dve.wait_ge(p3_exp, t - 2)
                    nc.vector.tensor_tensor(Z[:, t - 3, :], Z[:, t - 3, :], AT[:, t - 3, 0:N], ALU.mult).then_inc(p3_ready, 1)
            dve.wait_ge(num3_mm, 1)
            nc.vector.reciprocal(RDEN[:, 0:TA], VA[:, :, D])
            link(nc.vector.reciprocal(RDEN[:, TA:T], VB[:, :, D]))
            nc.vector.tensor_tensor(NRM[:, 0:TA, :], VA[:, :, 0:D], wide(RDEN[:, 0:TA], TA), ALU.mult)
            link(nc.vector.tensor_tensor(NRM[:, TA:T, :], VB[:, :, 0:D], wide(RDEN[:, TA:T], T - TA), ALU.mult))
            nc.vector.tensor_scalar(CEN[:, :, :], NRM[:, :, :], 0.0, None, ALU.min).then_inc(elu_in, 1)
            link(nc.vector.tensor_scalar(RES[:, :, :], NRM[:, :, :], 0.0, None, ALU.max))
            dve.wait_ge(elu_exp, 1)
            link(nc.vector.scalar_tensor_tensor(NRM[:, :, :], SQ[:, :, :], -1.0, RES[:, :, :], ALU.add, ALU.add))
            link(nc.vector.tensor_tensor(NRM[:, :, :], NRM[:, :, :], X[3][:, :, :], ALU.add))
            layer_norm(NRM, Y, 0, T).then_inc(x_ready, 1)

        @block.tensor
        def _(pe):
            mm, tr = nc.tensor.matmul, nc.tensor.transpose

            pe.wait_ge(idents, 3)
            pe.wait_ge(x_in, 32)
            for t in range(T):
                ins = tr(PSflat[0:D, t * P:(t + 1) * P], X[0][:, t, :], IDF[:, :])
            ins.then_inc(x0t_mm, 1)
            pe.wait_ge(w_in, 7 * 16)
            pe.wait_ge(wb_in, 11 * 16)
            for c in range(4):
                tr(PS[:, 3, c * W2:(c + 1) * W2], QS[:, c * P:(c + 1) * P], IDF[0:W2, 0:W2])
                tr(PS[:, 4, c * W2:(c + 1) * W2], KS[:, c * P:(c + 1) * P], IDF[0:W2, 0:W2])
            for h in range(H):
                tr(PS[0:D, 6 + h // 4, h % 4 * W2:(h % 4 + 1) * W2], VS[:, h * D:(h + 1) * D], IDF[0:W2, 0:W2])
            tr(PS[0:D, 5, 0:D], W3S[0:D, 0:D], IDF[0:D, 0:D]).then_inc(wts_mm, 1)

            pe.wait_ge(x0t_sb, 1)
            pe.wait_ge(wts_sb, 3)
            for c, w in PADDED:
                mm(PSflat[0:D, c:c + w], FC1[:, :], XT[0:D, c:c + w], start=True, stop=True)
            mm(PS[0:D, 5, 100:101], FC2[:, :], XT[0:D, 1:2], start=True, stop=True).then_inc(hid_mm, 1)

            for half in range(2):
                for c in range(4):
                    mm(PS[0:W2, 6, half * 2 * H:(half + 1) * 2 * H], QKT[:, 4 * half + c, :],
                       AW[:, 4 * half + c, :, :].rearrange("p k h -> p (k h)"), start=c == 0, stop=c == 3)
            for h in range(H):
                mm(PS[0:W2, 7, h * D:(h + 1) * D], VWT[:, h, :], PWS[:, h, :], start=True, stop=True)
            mm(PS[0:D, 3, 0:2], WT[:, :], A3[:, :], start=True, stop=True).then_inc(fold_mm, 1)

            pe.wait_ge(hid_sb, 1)
            for t in range(T):
                ins = mm(PS[:, 5, 128 + t:129 + t], HS[:, t * P:(t + 1) * P], ATW[:, :], start=True, stop=True)
            ins.then_inc(score_mm, 1)

            pe.wait_ge(fold_sb, 1)
            pe.wait_ge(score_dif, 1)
            pe.wait_ge(xs_ready, 1)
            pe.wait_ge(consts, 3)
            with pe.Fori(0, T) as it:
                pe.wait_ge(an_ready, it + 1)
                for j in range(T):
                    ins = tr(PSTR[:, j * P:(j + 1) * P], AN[:, bass.ds(it, 1), j * P:(j + 1) * P].rearrange("p a j -> p (a j)"), IDB[:, :])
                ins.then_inc(at_mm, 1)
                pe.wait_ge(at_lo, it + 1)
                pe.wait_ge(at_hi, it + 1)
                for j in range(T):
                    ins = mm(PSN[:, bass.ds(it, 1), 0:W0].rearrange("p a n -> p (a n)"),
                             AT[:, j, bass.ds(it * P, P)], XS[0][:, j, :], start=j == 0, stop=j == T - 1)
                ins.then_inc(sum0_mm, 1)

            pe.wait_ge(x_ready, len(GROUPS))
            with pe.Fori(0, T) as it:
                for j in range(T):
                    ins = mm(PSN[:, bass.ds(it, 1), 0:3 * D].rearrange("p a n -> p (a n)"),
                             AT[:, j, bass.ds(it * P, P)], XS[1][:, j, 0:3 * D], start=j == 0, stop=j == T - 1)
                ins.then_inc(sum1_mm, 1)

            def x_transposed(first, src, after):
                for n, (lo, hi) in enumerate(GROUPS):
                    pe.wait_ge(x_ready, len(GROUPS) * (first + 1) + n + 1)
                    if n == 2:
                        pe.wait_ge(xt_sb, len(GROUPS) * first + 1)
                    for t in range(lo, hi):
                        ins = tr(PS[0:D, 6 + n % 2, (t - lo) * P:(t - lo + 1) * P], src[:, t, :], IDF[:, :])
                    ins.then_inc(xt_mm, 1)
                for n, (c, w) in enumerate(CHUNKS):
                    pe.wait_ge(xt_sb, len(GROUPS) * first + n + 1)
                    after(n, c, w)

            x_transposed(0, X[2], lambda n, c, w: mm(PSflat[0:4 * H, c:c + w], W32[:, :], XT[:, c:c + w], start=True, stop=True).then_inc(ab_mm, 1))
            for t in range(T):
                ins = mm(PS[:, 3, 64 + t * H:64 + (t + 1) * H], XT[:, t * P:(t + 1) * P], W32[:, 2 * H:3 * H], start=True, stop=True)
            ins.then_inc(b0_mm, 1)
            pe.wait_ge(mxr_ready, 1)
            mm(PS[:, 4, 0:4 * H], MXR[:, :], IDF[0:4 * H, 0:4 * H], start=True, stop=True).then_inc(max_mm, 1)

            def row(h, half):
                for c in range(0, HALF, 512):
                    w = min(512, HALF - c)
                    ins = mm(MISC[:, c:c + w], SEL[:, :],
                             RHS1[:, bass.ds(h, 1), half * HALF + c:half * HALF + c + w].rearrange("p a n -> p (a n)"), start=True, stop=True)
                ins.then_inc(row_mm, 1)

            def values(h):
                for t in range(T):
                    ins = mm(v_block(t), XT[:, t * P:(t + 1) * P], VP[:, bass.ds(h, 1), :].rearrange("p a n -> p (a n)"), start=True, stop=True)
                ins.then_inc(val_mm, 1)

            def z1(h, t):
                for c, w in CHUNKS:
                    ins = mm(ZP[:, c:c + w], LHS1[:, bass.ds(h, 1), t * P:(t + 1) * P].rearrange("p a n -> p (a n)"),
                             RHS1[:, bass.ds(h, 1), c:c + w].rearrange("p a n -> p (a n)"), start=True, stop=True)
                ins.then_inc(z1_mm, 1)

            def weigh(h, t, par, first):
                k = rows_of(t)
                pe.wait_ge(p_ready, h * T + t + 1)
                for n, (c, w) in enumerate(CHUNKS):
                    if t == 0 and not first:
                        pe.wait_ge(acc_sb, 3 * (h - 1) + n + 1)
                    ins = mm(ACC[0:W2, c:c + w], VST[par][0:k, t, :], Z[0:k, t, c:c + w], start=t == 0, stop=t == T - 1)
                    if t == T - 1:
                        ins.then_inc(acc_mm, 1)
                    if n == len(CHUNKS) - 1 and t < T - 1:
                        ins.then_inc(p_used, 1)
                if t == T - 1:
                    pe.sem_inc(p_used, 1)

            def sums_back(h):
                pe.wait_ge(acc_sb, 3 * h + 3)
                for t in range(T):
                    ins = tr(v_block(t), NUMT[:, t * P:(t + 1) * P], IDF[0:W2, 0:W2])
                ins.then_inc(num_mm, 1)

            def head(h, par, first, last):
                for t in range(T):
                    pe.wait_ge(z_ready, h * T + t + 1)
                    if t < T - 1:
                        z1(h, t + 1)
                    elif not last:
                        z1(h + 1, 0)
                    if t >= 3:
                        weigh(h, t - 3, par, first)
                    elif not first:
                        weigh(h - 1, T - 3 + t, 1 - par, False)
                    if t == 4 and not first:
                        pe.wait_ge(val_sb, h + 1)
                        sums_back(h - 1)
                    if not last:
                        if t == 6:
                            if not first:
                                pe.wait_ge(num_added, h)
                            row(h + 1, 0)
                        if t == 7:
                            pe.wait_ge(row_sb, 2 * (h + 1) + 1)
                            row(h + 1, 1)
                        if t == 8:
                            pe.wait_ge(row_sb, 2 * (h + 1) + 2)
                            values(h + 1)

            pe.wait_ge(third_in, 9 * 16)
            pe.wait_ge(consts, 7)
            row(0, 0)
            pe.wait_ge(row_sb, 1)
            row(0, 1)
            pe.wait_ge(guards, 1)
            z1(0, 0)
            pe.wait_ge(row_sb, 2)
            values(0)
            pe.wait_ge(val_sb, 1)
            head(0, 0, True, False)
            with pe.Fori(0, H // 2 - 1) as pair:
                head(2 * pair + 1, 1, False, False)
                head(2 * pair + 2, 0, False, False)
            head(H - 1, 1, False, True)
            for t in range(T - 3, T):
                weigh(H - 1, t, 1, False)
            sums_back(H - 1)

            def f_row(n, c, w):
                ins = mm(ACC[:, c:c + w], FREP[:, :], XT[0:D, c:c + w], start=True, stop=True)
                if n == len(CHUNKS) - 1:
                    ins.then_inc(fg_mm, 1)
            pe.wait_ge(acc_sb, 3 * H)
            pe.wait_ge(num_added, H)
            x_transposed(1, X[3], f_row)
            for c, w in CHUNKS:
                ins = mm(ZP[:, c:c + w], GREP[:, :], XT[0:D, c:c + w], start=True, stop=True)
            ins.then_inc(fg_mm, 1)
            for t in range(T):
                ins = mm(wh_block(t), XT[:, t * P:(t + 1) * P], W3S[:, :], start=True, stop=True)
            ins.then_inc(wh_mm, 1)
            pe.wait_ge(wh_sb, 1)
            pe.wait_ge(guard3, 1)
            for t in range(T):
                k = rows_of(t)
                pe.wait_ge(p3_ready, t + 1)
                for c, w in CHUNKS:
                    ins = mm(ZP[0:W2, c:c + w], WH[0:k, t, 0:W2], Z[0:k, t, c:c + w], start=t == 0, stop=t == T - 1)
                    if t == T - 1:
                        ins.then_inc(acc3_mm, 1)
            pe.wait_ge(acc3_sb, len(CHUNKS))
            for t in range(T):
                ins = tr(v_block(t), NUMT[:, t * P:(t + 1) * P], IDF[0:W2, 0:W2])
            ins.then_inc(num3_mm, 1)


_INS = ['x', 'adj', 'L0_gnn_fc_w', 'L0_gnn_fc_b', 'L0_gnn_attn_w', 'L0_gnn_attn_b', 'L2_gnn_Qw', 'L2_gnn_Qb',
        'L2_gnn_Kw', 'L2_gnn_Kb', 'L2_gnn_Vw', 'L2_gnn_Vb', 'L2_gnn_a', 'L2_gnn_Pw', 'L2_gnn_Pb', 'L3_gnn_W', 'L3_gnn_a']


def kernel(**inputs):
    import concourse.bacc as _bacc
    from concourse.bass_utils import run_bass_kernel_spmd as _run

    nc = _bacc.Bacc("TRN2", target_bir_lowering=False, num_devices=1)
    arrays, args = {}, []
    for name in _INS:
        arr = np.ascontiguousarray(inputs[name])
        arrays[f"in_{name}_dram"] = arr
        args.append(nc.dram_tensor(f"in_{name}_dram", arr.shape, mybir.dt.from_np(arr.dtype), kind="ExternalInput").ap())
    args.append(nc.dram_tensor("out_dram", (N, D), F32, kind="ExternalOutput").ap())
    graph_kernel(nc, *args)
    r = _run(nc, [arrays], core_ids=[0])
    return r.results[0]["out_dram"]
```

```python
from contextlib import ExitStack

import numpy as np
import concourse.bass as bass
from concourse import mybir
from concourse.alu_op_type import AluOpType as ALU

ACT = mybir.ActivationFunctionType
F32 = mybir.dt.float32
BF16 = mybir.dt.bfloat16
I32 = mybir.dt.int32
U16 = mybir.dt.uint16
X_AXIS = mybir.AxisListType.X

P = 128
N, D = 1354, 64
T = -(-N // P)
NP = T * P
LAST = N - (T - 1) * P
H = 8
DH = H * D
EPS = 1e-5
CHUNKS = [(c, min(512, N - c)) for c in range(0, N, 512)]
PADDED = [(c, min(512, NP - c)) for c in range(0, NP, 512)]
HALF = N // 2
GROUPS = [(0, 4), (4, 8), (8, T)]
W0 = 3 * D + 1
W2 = D + 1
W3 = D + 3
STAGES = 5
TA = 7


def rows_of(t):
    return LAST if t == T - 1 else P


def graph_kernel(nc, x, adj, fc_w, fc_b, attn_w, attn_b, Qw, Qb, Kw, Kb, Vw, Vb, a, Pw, Pb, W, a3, out):
    with ExitStack() as ctx:
        def sb(name, shape, dt=F32):
            return ctx.enter_context(nc.sbuf_tensor(name, shape, dt))

        def sem(name):
            return ctx.enter_context(nc.semaphore(name))

        AT = sb("AT", [P, T, NP], BF16)
        Z = sb("Z", [P, T, N])
        Zflat = Z[:, :, :].rearrange("p t n -> p (t n)")
        AN_WORDS = T * NP // 2
        AN = Zflat[:, 0:AN_WORDS].bitcast(BF16).rearrange("p (t n) -> p t n", t=T)
        STAGE = Zflat[:, AN_WORDS:AN_WORDS + STAGES * N].bitcast(I32).rearrange("p (s n) -> p s n", s=STAGES)
        X = [sb(f"X{i}", [P, T, D]) for i in range(4)]
        XS = [sb(f"XS{i}", [P, T, W0], BF16) for i in range(2)]
        RES = sb("RES", [P, T, D])
        Y = sb("Y", [P, T, D])
        CEN = sb("CEN", [P, T, D])
        SQ = sb("SQ", [P, T, D])
        STAT = sb("STAT", [P, 8, T])
        XT = sb("XT", [W2, NP])
        NUMT = sb("NUMT", [W2, NP])
        TERMS = sb("TERMS", [P, N], BF16)
        PICK0 = sb("PICK0", [P, H, P], BF16)
        LHS1 = sb("LHS1", [P, H, NP], BF16)
        SEL = sb("SEL", [P, 2, H], BF16)
        SELF = sb("SELF", [P, 2, H])
        ROW0 = [sb(f"ROW0_{i}", [P, N]) for i in range(2)]
        VST = [sb(f"VST{i}", [P, T, W2]) for i in range(2)]
        B0 = sb("B0", [P, T, H])
        NEGC = sb("NEGC", [P, H])
        AB = Z[0:4 * H, T - 1, :]
        R1 = Z[0:4 * H, T - 2, :]
        MID = Z[0:4 * H, T - 3, :].bitcast(BF16)[:, 0:N]
        WH = sb("WH", [P, T, W3])
        IDF = sb("IDF", [P, P])
        IDB = sb("IDB", [P, P], BF16)
        ONES = sb("ONES", [P, P])
        QS, KS = ROW0[0][0:W2, 0:DH], ROW0[0][0:W2, DH:2 * DH]
        VS = ROW0[1][0:W2, 0:DH]
        QKT = ROW0[1][:, DH:DH + 8 * W2].rearrange("p (c d) -> p c d", d=W2)
        VWT = VST[0][0:D, 0:H, :]
        PWS = VST[1][0:D, 0:H, 0:D]
        AW = sb("AW", [P, 8, 2, H])
        W32 = sb("W32", [W2, 4 * H])
        VP = sb("VP", [W2, H, W2])
        W3S = sb("W3S", [W2, W3])
        A3 = sb("A3", [D, 2])
        WT = sb("WT", [D, D])
        WA3 = sb("WA3", [D, 2])
        FREP = sb("FREP", [D, P])
        FC1 = sb("FC1", [W2, D])
        FC2 = sb("FC2", [D, D])
        X1R = sb("X1R", [D, P])
        NEIGH = sb("NEIGH", [P, D])
        ATW = sb("ATW", [P, D])
        ATB = sb("ATB", [P, 1])
        PBB = sb("PBB", [P, D])
        SC = sb("SC", [P, 3, T])
        WROW = sb("WROW", [P, T])
        MX = sb("MX", [4 * H, 4])
        MXR = sb("MXR", [4 * H, P])
        G2 = sb("G2", [P, 3, 2 * H])
        RDEN = sb("RDEN", [P, T])
        NRM = sb("NRM", [P, T, D])
        MX3 = sb("MX3", [P, 3])
        MX3T = sb("MX3T", [3, P + 1])
        C3 = sb("C3", [P, 5])
        R3 = ROW0[0]
        S3 = sb("S3", [P, T])
        V3 = sb("V3", [P, T])

        PS = ctx.enter_context(nc.psum_tensor("PS", [P, 8, 512], F32))
        PSflat = PS[:, :, :].rearrange("p b n -> p (b n)")
        PSN = PSflat[:, 0:3072].rearrange("p (t n) -> p t n", n=256)
        PSTR = PSflat[:, 3072:4096].bitcast(BF16)
        ACC = PSflat[:, 0:N]
        ZP = PSflat[:, 1536:1536 + N]
        MISC = PSflat[:, 3072:4096]

        def two_banks(bank, width):
            return (PS[:, bank, 0:TA * width].rearrange("p (t n) -> p t n", n=width),
                    PS[:, bank + 1, 0:(T - TA) * width].rearrange("p (t n) -> p t n", n=width),
                    lambda t: PS[:, bank + t // TA, t % TA * width:t % TA * width + width])

        VA, VB, v_block = two_banks(6, W2)
        WHA, WHB, wh_block = two_banks(3, W3)

        x_in, w_in, wb_in = sem("x_in"), sem("w_in"), sem("wb_in")
        adj_in = [sem(f"adj_in{t}") for t in range(T)]
        w3_zero = sem("w3_zero")
        consts, x_pad, idents, an_pads = sem("consts"), sem("x_pad"), sem("idents"), sem("an_pads")
        terms_set, sel_step, lhs_set, b1_in = sem("terms_set"), sem("sel_step"), sem("lhs_set"), sem("b1_in")
        hi_ready, mid_ready, lo_ready, r1_ready = sem("hi_ready"), sem("mid_ready"), sem("lo_ready"), sem("r1_ready")
        x0t_mm, x0t_sb, wts_mm, wts_sb = sem("x0t_mm"), sem("x0t_sb"), sem("wts_mm"), sem("wts_sb")
        fold_mm, fold_sb, hid_mm = sem("fold_mm"), sem("fold_sb"), sem("hid_mm")
        score_dif, score_exp = sem("score_dif"), sem("score_exp")
        xs_ready, an_ready, at_mm, at_lo, at_hi = sem("xs_ready"), sem("an_ready"), sem("at_mm"), sem("at_lo"), sem("at_hi")
        sum0_mm, sum1_mm = sem("sum0_mm"), sem("sum1_mm")
        var_ready, rstd_ready, x_ready = sem("var_ready"), sem("rstd_ready"), sem("x_ready")
        xt_mm, xt_sb = sem("xt_mm"), sem("xt_sb")
        ab_mm, ab_sb = sem("ab_mm"), sem("ab_sb")
        b0_mm, mxr_ready, max_mm, guards = sem("b0_mm"), sem("mxr_ready"), sem("max_mm"), sem("guards")
        row_mm, row_sb, val_mm, val_sb = sem("row_mm"), sem("row_sb"), sem("val_mm"), sem("val_sb")
        tiles_picked = sem("tiles_picked")
        z0_ready, z1_mm, z_ready = sem("z0_ready"), sem("z1_mm"), sem("z_ready")
        leaky_ready, p_ready, p_used = sem("leaky_ready"), sem("p_ready"), sem("p_used")
        acc_mm, acc_sb, num_mm, num_added, norm_step = sem("acc_mm"), sem("acc_sb"), sem("num_mm"), sem("num_added"), sem("norm_step")
        wh_mm, wh_sb, guard3 = sem("wh_mm"), sem("wh_sb"), sem("guard3")
        f_rows, f_mm, max3_ready, max3_mm = sem("f_rows"), sem("f_mm"), sem("max3_ready"), sem("max3_mm")
        v3_exp, r3_exp, pb_in, atw_in, x1_rows = sem("v3_exp"), sem("r3_exp"), sem("pb_in"), sem("atw_in"), sem("x1_rows")
        waits_done = sem("waits_done")
        p3_ready, acc3_mm, acc3_sb, num3_mm = sem("p3_ready"), sem("acc3_mm"), sem("acc3_sb"), sem("num3_mm")
        elu_in, elu_exp, out_done = sem("elu_in"), sem("elu_exp"), sem("out_done")

        block = ctx.enter_context(nc.Block())

        @block.sync
        def _(sp):
            sp.wait_ge(x_pad, 1)
            sp.dma_start(X[0][:, 0:T - 1, :], x[0:(T - 1) * P, :].rearrange("(t p) d -> p t d", p=P)).then_inc(x_in, 16)
            sp.dma_start(X[0][0:LAST, T - 1, :], x[(T - 1) * P:N, :]).then_inc(x_in, 16)
            for t in range(T):
                if t >= STAGES:
                    sp.wait_ge(an_ready, t - STAGES + 1)
                sp.dma_start(STAGE[0:rows_of(t), t % STAGES, :], adj[t * P:t * P + rows_of(t), :]).then_inc(adj_in[t], 16)
            sp.wait_ge(lhs_set, H)
            for n, (c, w) in enumerate(CHUNKS):
                for s, ready in enumerate((hi_ready, mid_ready, lo_ready)):
                    sp.wait_ge(ready, n + 1)
                    sp.dma_start(LHS1[96 + s:97 + s, :, c:c + w], TERMS[32 * s + 3 * H:32 * s + 4 * H, c:c + w]).then_inc(b1_in, 16)
            sp.wait_ge(x_ready, 3 * len(GROUPS) + 1)
            sp.dma_start(out[0:(T - 1) * P, :].rearrange("(t p) d -> p t d", p=P), Y[:, 0:T - 1, :]).then_inc(out_done, 16)
            sp.dma_start(out[(T - 1) * P:N, :], Y[0:LAST, T - 1, :]).then_inc(out_done, 16)
            sp.wait_ge(out_done, 32)

        @block.gpsimd
        def _(pool):
            count = {}

            def alone(ins, signal):
                count[signal.name] = count.get(signal.name, 0) + 1
                ins.then_inc(signal, 1)
                pool.wait_ge(signal, count[signal.name])

            alone(nc.gpsimd.memset(X[0][:, T - 1, :], 0.0), x_pad)
            alone(nc.gpsimd.memset(ONES[:, :], 1.0), idents)
            alone(nc.gpsimd.affine_select(out=IDF[:, :], in_=ONES[:, :], compare_op=ALU.is_equal, fill=0.0, base=0,
                                          pattern=[[-1, P]], channel_multiplier=1), idents)
            alone(nc.gpsimd.tensor_copy(IDB[:, :], IDF[:, :]), idents)
            alone(nc.gpsimd.memset(XT[D:W2, :], 1.0), consts)
            alone(nc.gpsimd.memset(XS[0][:, :, W0 - 1:W0], 1.0), consts)
            alone(nc.gpsimd.memset(AN[:, :, N:NP], 0.0), an_pads)
            alone(nc.gpsimd.memset(AN[:, T - 1, 0:N], 1.0), an_pads)
            for dst, weight, bias in ((QS, Qw, Qb), (KS, Kw, Kb), (VS, Vw, Vb)):
                pool.dma_start(dst[0:D, :], weight).then_inc(w_in, 16)
                pool.dma_start(dst[D:W2, :], bias.unsqueeze(0)).then_inc(w_in, 16)
            pool.dma_start(PWS[:, :, :], Pw.rearrange("(h d) o -> d h o", d=D)).then_inc(w_in, 16)
            pool.dma_start(A3[:, 0:1], a3[0:D, :]).then_inc(w_in, 16)
            pool.dma_start(A3[:, 1:2], a3[D:2 * D, :]).then_inc(w_in, 16)
            for k in range(2):
                pool.dma_start(AW[:, :, k, :], a[k].rearrange("(c p) h -> p c h", p=P)).then_inc(w_in, 16)
            pool.dma_start(PBB[:, :], Pb.partition_broadcast(P)).then_inc(pb_in, 16)
            alone(nc.gpsimd.memset(W3S[:, :], 0.0), w3_zero)
            pool.dma_start(W3S[0:D, 0:D], W).then_inc(w_in, 16)
            alone(nc.gpsimd.memset(W3S[D:W2, D:D + 1], 1.0), consts)
            alone(nc.gpsimd.memset(VP[:, :, D:W2], 0.0), consts)
            alone(nc.gpsimd.memset(VP[D:W2, :, D:W2], 1.0), consts)
            alone(nc.gpsimd.memset(TERMS[96:P, :], 1.0), terms_set)
            for k in range(2):
                alone(nc.gpsimd.tensor_tensor(SELF[:, k, :], IDF[:, k * H:(k + 1) * H], IDF[:, 32 + k * H:32 + (k + 1) * H], ALU.add), sel_step)
                alone(nc.gpsimd.tensor_tensor(SEL[:, k, :], SELF[:, k, :], IDF[:, 64 + k * H:64 + (k + 1) * H], ALU.add), sel_step)
            alone(nc.gpsimd.tensor_copy(PICK0[:, :, :], SEL[:, 0, :].unsqueeze(2).to_broadcast([P, H, P])), terms_set)
            for n in range(3 * len(GROUPS) + 1):
                if n == 2 * len(GROUPS):
                    for h in range(H):
                        pool.wait_ge(norm_step, 2 * h + 2)
                        alone(nc.gpsimd.tensor_tensor(Y[:, :, :], Y[:, :, :], NRM[:, :, :], ALU.add), num_added)
                g = GROUPS[n % len(GROUPS)] if n < 3 * len(GROUPS) else (0, T)
                pool.wait_ge(var_ready, n + 1)
                alone(nc.gpsimd.tensor_tensor(STAT[:, 3, g[0]:g[1]], STAT[:, 2, g[0]:g[1]], STAT[:, 7, g[0]:g[1]],
                                              ALU.pow), rstd_ready)

        @block.scalar
        def _(act):
            act.dma_start(FC1[0:D, :], fc_w[0:D, :]).then_inc(wb_in, 16)
            act.dma_start(FC1[D:W2, :], fc_b.unsqueeze(0)).then_inc(wb_in, 16)
            act.dma_start(FC2[:, :], fc_w[D:2 * D, :]).then_inc(wb_in, 16)
            act.dma_start(ATW[:, :], attn_w.rearrange("d o -> (d o)").partition_broadcast(P)).then_inc(atw_in, 16)
            act.dma_start(ATB[:, :], attn_b.partition_broadcast(P)).then_inc(atw_in, 16)
            act.wait_ge(x0t_mm, 1)
            nc.scalar.activation(XT[0:D, :], PSflat[0:D, 0:NP], ACT.Copy).then_inc(x0t_sb, 1)

            act.wait_ge(an_pads, 2)
            for t in range(T):
                if t == 2:
                    act.wait_ge(score_dif, 1)
                    nc.scalar.activation(WROW[:, :], SC[:, 2, :], ACT.Exp).then_inc(score_exp, 1)
                act.wait_ge(adj_in[t], 16)
                nc.scalar.activation(AN[0:rows_of(t), t, 0:N], STAGE[0:rows_of(t), t % STAGES, :], ACT.Copy).then_inc(an_ready, 1)
                if t >= T - H:
                    h = t - (T - H)
                    act.wait_ge(sel_step, 4)
                    nc.scalar.activation(LHS1[:, h, :], SEL[:, 1, h:h + 1].to_broadcast([P, NP]), ACT.Copy).then_inc(lhs_set, 1)
                if t >= 1:
                    act.wait_ge(at_mm, t)
                    nc.scalar.activation(AT[:, 8:T, (t - 1) * P:t * P], PSTR[:, 8 * P:T * P].rearrange("p (j i) -> p j i", i=P), ACT.Copy).then_inc(at_hi, 1)
            act.wait_ge(at_mm, T)
            nc.scalar.activation(AT[:, 8:T, (T - 1) * P:NP], PSTR[:, 8 * P:T * P].rearrange("p (j i) -> p j i", i=P), ACT.Copy).then_inc(at_hi, 1)

            act.wait_ge(wts_mm, 1)
            nc.scalar.activation(QKT[:, 0:4, :], PS[:, 6, 0:4 * W2].rearrange("p (c d) -> p c d", d=W2), ACT.Copy)
            nc.scalar.activation(QKT[:, 4:8, :], PS[:, 7, 0:4 * W2].rearrange("p (c d) -> p c d", d=W2), ACT.Copy)
            nc.scalar.activation(WT[:, :], PS[0:D, 2, 0:D], ACT.Copy)
            for half in range(2):
                ins = nc.scalar.activation(VWT[:, 4 * half:4 * half + 4, :], PS[0:D, half, 0:4 * W2].rearrange("p (h d) -> p h d", d=W2), ACT.Copy)
            ins.then_inc(wts_sb, 1)
            act.wait_ge(fold_mm, 1)
            nc.scalar.activation(W32[:, :], PS[0:W2, 3, 0:4 * H], ACT.Copy)
            nc.scalar.activation(W3S[0:D, D + 1:D + 2], PS[0:D, 3, 65:66], ACT.Copy)
            nc.scalar.activation(W3S[0:D, D + 2:D + 3], PS[0:D, 3, 64:65], ACT.Copy)
            nc.scalar.activation(WA3[:, :], PS[0:D, 3, 64:66], ACT.Copy)
            nc.scalar.activation(VP[:, :, 0:D], PS[0:W2, 6, :].rearrange("p (h d) -> p h d", d=D), ACT.Copy).then_inc(fold_sb, 1)

            def xt_copy(layer, n):
                lo, hi = GROUPS[n]
                act.wait_ge(xt_mm, layer * len(GROUPS) + n + 1)
                nc.scalar.activation(XT[0:D, lo * P:hi * P], PS[0:D, 6 + n % 2, 0:(hi - lo) * P], ACT.Copy).then_inc(xt_sb, 1)

            for n, (c, w) in enumerate(CHUNKS):
                xt_copy(0, n)
                act.wait_ge(ab_mm, n + 1)
                nc.scalar.activation(AB[:, c:c + w], PSflat[0:4 * H, c:c + w], ACT.Copy).then_inc(ab_sb, 1)
            for n, (c, w) in enumerate(CHUNKS):
                act.wait_ge(r1_ready, n + 1)
                nc.scalar.activation(TERMS[32:64, c:c + w], R1[:, c:c + w], ACT.Copy).then_inc(mid_ready, 1)

            def row_copy(h, half, par):
                act.wait_ge(row_mm, 2 * h + half + 1)
                nc.scalar.activation(ROW0[par][:, half * HALF:(half + 1) * HALF], MISC[:, 0:HALF], ACT.Copy).then_inc(row_sb, 1)

            def val_copy(h, par):
                act.wait_ge(val_mm, h + 1)
                nc.scalar.activation(VST[par][:, 0:TA, :], VA, ACT.Copy)
                nc.scalar.activation(VST[par][:, TA:T, :], VB, ACT.Copy).then_inc(val_sb, 1)

            def z0(h, t, par, reused):
                if t == 0:
                    act.wait_ge(row_sb, 2 * h + 2)
                if reused:
                    act.wait_ge(p_used, (h - 1) * T + t + 1)
                act.sem_inc(waits_done, 1)
                nc.scalar.activation(Z[:, t, :], ROW0[par][:, :], ACT.Identity, bias=B0[:, t, bass.ds(h, 1)]).then_inc(z0_ready, 1)

            def exp(h, t):
                act.wait_ge(leaky_ready, h * T + t + 1)
                act.sem_inc(waits_done, 1)
                nc.scalar.activation(Z[:, t, :], Z[:, t, :], ACT.Exp, bias=NEGC[:, bass.ds(h, 1)]).then_inc(p_ready, 1)

            def sums_copy(h):
                for n, (c, w) in enumerate(CHUNKS):
                    act.wait_ge(acc_mm, 3 * h + n + 1)
                    nc.scalar.activation(NUMT[:, c:c + w], ACC[0:W2, c:c + w], ACT.Copy).then_inc(acc_sb, 1)

            def head(h, par, first, last):
                for t in range(T):
                    if t == 3 and not first:
                        sums_copy(h - 1)
                    if t < T - 1:
                        z0(h, t + 1, par, not first)
                    elif not last:
                        z0(h + 1, 0, 1 - par, True)
                    if t >= 2:
                        exp(h, t - 2)
                    elif not first:
                        exp(h - 1, T - 2 + t)
                    if t == 1 and not first:
                        val_copy(h, par)
                    if not last:
                        if t in (7, 8):
                            row_copy(h + 1, t - 7, 1 - par)

            val_copy(0, 0)
            row_copy(0, 0, 0)
            row_copy(0, 1, 0)
            act.wait_ge(guards, 1)
            z0(0, 0, 0, False)
            head(0, 0, True, False)
            with act.Fori(0, H // 2 - 1) as pair:
                head(2 * pair + 1, 1, False, False)
                head(2 * pair + 2, 0, False, False)
            head(H - 1, 1, False, True)
            exp(H - 1, T - 2)
            exp(H - 1, T - 1)
            sums_copy(H - 1)

            for n in range(len(GROUPS)):
                xt_copy(1, n)
            act.wait_ge(wh_mm, 1)
            nc.scalar.activation(WH[:, 0:TA, :], WHA, ACT.Copy)
            nc.scalar.activation(WH[:, TA:T, :], WHB, ACT.Copy).then_inc(wh_sb, 1)
            act.wait_ge(guard3, 1)
            nc.scalar.activation(V3[:, :], WH[:, :, D + 1], ACT.Exp, bias=C3[:, 4:5]).then_inc(v3_exp, 1)
            nc.scalar.activation(S3[:, :], WH[:, :, D + 1], ACT.Exp, bias=C3[:, 3:4], scale=-0.8)
            act.wait_ge(f_mm, 1)
            nc.scalar.activation(R3[:, :], ACC, ACT.Exp, bias=C3[:, 3:4], scale=0.8).then_inc(r3_exp, 1)
            for n, (c, w) in enumerate(CHUNKS):
                act.wait_ge(acc3_mm, n + 1)
                nc.scalar.activation(NUMT[:, c:c + w], ZP[0:W2, c:c + w], ACT.Copy).then_inc(acc3_sb, 1)
            act.wait_ge(elu_in, 1)
            nc.scalar.activation(SQ[:, :, :], CEN[:, :, :], ACT.Exp).then_inc(elu_exp, 1)

        @block.vector
        def _(dve):
            done = [0]
            chain = sem("dve_chain")

            def link(ins):
                done[0] += 1
                ins.then_inc(chain, 1)
                dve.wait_ge(chain, done[0])

            def wide(ap, n):
                return ap.unsqueeze(2).to_broadcast([P, n, D])

            def thirds(src, dst, lo, hi):
                link(nc.vector.tensor_copy(dst[:, lo:hi, 0:D], src[:, lo:hi, :]))
                link(nc.vector.tensor_tensor(RES[:, lo:hi, :], src[:, lo:hi, :], dst[:, lo:hi, 0:D], ALU.subtract))
                link(nc.vector.tensor_copy(dst[:, lo:hi, D:2 * D], RES[:, lo:hi, :]))
                return nc.vector.tensor_tensor(dst[:, lo:hi, 2 * D:3 * D], RES[:, lo:hi, :], dst[:, lo:hi, D:2 * D], ALU.subtract)

            norms = [0]

            def layer_norm(src, dst, lo, hi):
                n = hi - lo
                link(nc.vector.tensor_reduce(STAT[:, 0, lo:hi], src[:, lo:hi, :], X_AXIS, ALU.add))
                link(nc.vector.tensor_scalar(STAT[:, 1, lo:hi], STAT[:, 0, lo:hi], 1.0 / D, None, ALU.mult))
                link(nc.vector.tensor_tensor(CEN[:, lo:hi, :], src[:, lo:hi, :], wide(STAT[:, 1, lo:hi], n), ALU.subtract))
                link(nc.vector.tensor_tensor(SQ[:, lo:hi, :], CEN[:, lo:hi, :], CEN[:, lo:hi, :], ALU.mult))
                link(nc.vector.tensor_reduce(STAT[:, 4, lo:hi], SQ[:, lo:hi, :], X_AXIS, ALU.add))
                nc.vector.tensor_scalar(STAT[:, 2, lo:hi], STAT[:, 4, lo:hi], 1.0 / D, EPS, ALU.mult, ALU.add).then_inc(var_ready, 1)
                norms[0] += 1
                dve.wait_ge(rstd_ready, norms[0])
                return nc.vector.tensor_tensor(dst[:, lo:hi, :], CEN[:, lo:hi, :], wide(STAT[:, 3, lo:hi], n), ALU.mult)

            def sum_thirds(dst, lo, hi):
                link(nc.vector.tensor_reduce(dst[:, lo:hi, :], PSN[:, lo:hi, 0:3 * D].rearrange("p t (s d) -> p t d s", s=3), X_AXIS, ALU.add))

            link(nc.vector.memset(STAT[:, 7, :], -0.5))
            link(nc.vector.memset(NUMT[:, :], 1.0))

            dve.wait_ge(x_in, 32)
            thirds(X[0], XS[0], 0, T).then_inc(xs_ready, 1)
            dve.wait_ge(x0t_sb, 1)
            nc.vector.tensor_scalar(X1R[:, :], ONES[0:D, :], XT[0:D, 1:2], None, ALU.mult).then_inc(x1_rows, 1)
            dve.wait_ge(hid_mm, 1)
            link(nc.vector.tensor_copy(NEIGH[:, :], PS[:, 5, 0:D]))
            link(nc.vector.tensor_tensor(CEN[:, :, :], PSflat[:, 3 * 512:3 * 512 + T * D].rearrange("p (t d) -> p t d", d=D), NEIGH[:, :].unsqueeze(1).to_broadcast([P, T, D]), ALU.add))
            link(nc.vector.scalar_tensor_tensor(SQ[:, :, :], CEN[:, :, :], 0.01, CEN[:, :, :], ALU.mult, ALU.max))
            dve.wait_ge(atw_in, 32)
            link(nc.vector.tensor_tensor(CEN[:, :, :], SQ[:, :, :], ATW[:, :].unsqueeze(1).to_broadcast([P, T, D]), ALU.mult))
            link(nc.vector.tensor_reduce(SC[:, 1, :], CEN[:, :, :], X_AXIS, ALU.add))
            link(nc.vector.tensor_scalar(SC[:, 0, :], SC[:, 1, :], ATB[:, 0:1], None, ALU.add))
            link(nc.vector.tensor_tensor(SC[:, 1, :], SC[:, 0, :], SC[:, 0, :], ALU.max))
            nc.vector.tensor_tensor(SC[:, 2, :], SC[:, 0, :], SC[:, 1, :], ALU.subtract).then_inc(score_dif, 1)

            def layer0(lo, hi):
                n = hi - lo
                dve.wait_ge(sum0_mm, hi)
                sum_thirds(NRM, lo, hi)
                link(nc.vector.tensor_tensor(RDEN[:, lo:hi], PSN[:, lo:hi, W0 - 1], WROW[:, lo:hi], ALU.mult))
                link(nc.vector.reciprocal(STAT[:, 5, lo:hi], RDEN[:, lo:hi]))
                link(nc.vector.tensor_tensor(STAT[:, 6, lo:hi], STAT[:, 5, lo:hi], WROW[:, lo:hi], ALU.mult))
                link(nc.vector.tensor_tensor(NRM[:, lo:hi, :], NRM[:, lo:hi, :], wide(STAT[:, 6, lo:hi], n), ALU.mult))
                link(nc.vector.tensor_tensor(Y[:, lo:hi, :], NRM[:, lo:hi, :], X[0][:, lo:hi, :], ALU.add))
                link(layer_norm(Y, X[1], lo, hi))
                thirds(X[1], XS[1], lo, hi).then_inc(x_ready, 1)

            for t in range(T):
                if t == 4:
                    dve.wait_ge(score_exp, 1)
                dve.wait_ge(at_mm, t + 1)
                nc.vector.tensor_copy(AT[:, 0:8, t * P:(t + 1) * P], PSTR[:, 0:8 * P].rearrange("p (j i) -> p j i", i=P)).then_inc(at_lo, 1)
                for lo, hi in GROUPS[:-1]:
                    if t == hi:
                        layer0(lo, hi)
            layer0(*GROUPS[-1])

            def ab_thirds(n):
                c, w = CHUNKS[n]
                dve.wait_ge(ab_sb, n + 1)
                nc.vector.tensor_copy(TERMS[0:32, c:c + w], AB[:, c:c + w]).then_inc(hi_ready, 1)
                dve.wait_ge(hi_ready, n + 1)
                nc.vector.tensor_tensor(R1[:, c:c + w], AB[:, c:c + w], TERMS[0:32, c:c + w], ALU.subtract).then_inc(r1_ready, 1)
                dve.wait_ge(r1_ready, n + 1)
                link(nc.vector.tensor_copy(MID[:, c:c + w], R1[:, c:c + w]))
                nc.vector.tensor_tensor(TERMS[64:96, c:c + w], R1[:, c:c + w], MID[:, c:c + w], ALU.subtract).then_inc(lo_ready, 1)
                link(nc.vector.tensor_reduce(MX[:, n:n + 1], AB[:, c:c + w], X_AXIS, ALU.max))

            for lo, hi in GROUPS:
                dve.wait_ge(sum1_mm, hi)
                sum_thirds(NRM, lo, hi)
                link(nc.vector.scalar_tensor_tensor(Y[:, lo:hi, :], X[1][:, lo:hi, :], 2.0, NRM[:, lo:hi, :], ALU.mult, ALU.add))
                layer_norm(Y, X[2], lo, hi).then_inc(x_ready, 1)
            for n in range(len(CHUNKS)):
                ab_thirds(n)

            dve.wait_ge(at_hi, T)
            link(nc.vector.tensor_reduce(MX[:, 3:4], MX[:, 0:3], X_AXIS, ALU.max))
            nc.vector.tensor_scalar(MXR[:, :], ONES[0:4 * H, :], MX[:, 3:4], None, ALU.mult).then_inc(mxr_ready, 1)
            dve.wait_ge(b0_mm, 1)
            link(nc.vector.tensor_copy(B0[:, :, :], PS[:, 3, 64:64 + T * H].rearrange("p (t h) -> p t h", h=H)))
            dve.wait_ge(max_mm, 1)
            link(nc.vector.tensor_copy(G2[:, 0, :], PS[:, 4, 0:2 * H]))
            link(nc.vector.tensor_tensor(G2[:, 1, :], PS[:, 4, 2 * H:4 * H], G2[:, 0, :], ALU.add))
            link(nc.vector.scalar_tensor_tensor(G2[:, 2, :], G2[:, 1, :], 0.2, G2[:, 1, :], ALU.mult, ALU.max))
            link(nc.vector.tensor_tensor(G2[:, 0, 0:H], G2[:, 2, 0:H], G2[:, 2, H:2 * H], ALU.max))
            nc.vector.tensor_scalar(NEGC[:, :], G2[:, 0, 0:H], -1.0, None, ALU.mult).then_inc(guards, 1)
            dve.wait_ge(fold_sb, 1)
            nc.vector.tensor_scalar(FREP[:, :], ONES[0:D, :], WA3[:, 0:1], None, ALU.mult).then_inc(f_rows, 1)
            dve.wait_ge(pb_in, 16)
            link(nc.vector.tensor_tensor(Y[:, :, :], X[2][:, :, :], PBB[:, :].unsqueeze(1).to_broadcast([P, T, D]), ALU.add))

            def pick(h, t):
                dve.wait_ge(z0_ready, h * T + t + 1)
                dve.wait_ge(z1_mm, h * T + t + 1)
                dve.sem_inc(tiles_picked, 1)
                nc.vector.copy_predicated(Z[:, t, :], AT[:, t, 0:N].bitcast(U16), ZP).then_inc(z_ready, 1)

            def leaky(h, t):
                dve.wait_ge(z_ready, h * T + t + 1)
                nc.vector.scalar_tensor_tensor(Z[:, t, :], Z[:, t, :], 0.2, Z[:, t, :], ALU.mult, ALU.max).then_inc(leaky_ready, 1)

            def normalise_head(h, first):
                dve.wait_ge(num_mm, h + 1)
                if not first:
                    dve.wait_ge(num_added, h)
                nc.vector.reciprocal(RDEN[:, 0:TA], VA[:, :, D])
                nc.vector.reciprocal(RDEN[:, TA:T], VB[:, :, D]).then_inc(norm_step, 1)
                dve.wait_ge(norm_step, 2 * h + 1)
                nc.vector.tensor_tensor(NRM[:, 0:TA, :], VA[:, :, 0:D], wide(RDEN[:, 0:TA], TA), ALU.mult)
                nc.vector.tensor_tensor(NRM[:, TA:T, :], VB[:, :, 0:D], wide(RDEN[:, TA:T], T - TA), ALU.mult).then_inc(norm_step, 1)

            def head(h, nth):
                for t in range(T):
                    pick(h, t)
                    if t > 0:
                        leaky(h, t - 1)
                    elif nth > 0:
                        leaky(h - 1, T - 1)
                    if t == 5 and nth > 0:
                        normalise_head(h - 1, nth == 1)

            head(0, 0)
            head(1, 1)
            with dve.Fori(2, H) as h:
                head(h, 2)
            leaky(H - 1, T - 1)
            normalise_head(H - 1, False)
            dve.wait_ge(num_added, H)
            for lo, hi in GROUPS:
                layer_norm(Y, X[3], lo, hi).then_inc(x_ready, 1)

            dve.wait_ge(wh_sb, 1)
            for col, n_op in ((0, D + 2), (1, D + 1)):
                nc.vector.tensor_reduce(MX3[:, col:col + 1], WH[:, 0:T - 1, n_op], X_AXIS, ALU.max)
            link(nc.vector.tensor_reduce(MX3[:, 2:3], WH[:, 0:T - 1, D + 1], X_AXIS, ALU.min))
            nc.vector.tensor_tensor(MX3[0:LAST, 0:1], MX3[0:LAST, 0:1], WH[0:LAST, T - 1, D + 2:D + 3], ALU.max)
            nc.vector.tensor_tensor(MX3[0:LAST, 1:2], MX3[0:LAST, 1:2], WH[0:LAST, T - 1, D + 1:D + 2], ALU.max)
            link(nc.vector.tensor_tensor(MX3[0:LAST, 2:3], MX3[0:LAST, 2:3], WH[0:LAST, T - 1, D + 1:D + 2], ALU.min))
            nc.vector.tensor_scalar(MX3[:, 2:3], MX3[:, 2:3], -1.0, None, ALU.mult).then_inc(max3_ready, 1)
            dve.wait_ge(max3_mm, 1)
            link(nc.vector.tensor_reduce(MX3T[:, P:P + 1], PS[0:3, 6, 0:P], X_AXIS, ALU.max))
            nc.vector.tensor_scalar(MX3T[:, 0:P], ONES[0:3, :], MX3T[:, P:P + 1], None, ALU.mult).then_inc(max3_ready, 1)
            dve.wait_ge(max3_mm, 2)
            link(nc.vector.tensor_copy(C3[:, 0:3], PS[:, 6, 0:3]))
            link(nc.vector.tensor_tensor(C3[:, 3:4], C3[:, 0:1], C3[:, 2:3], ALU.max))
            nc.vector.tensor_scalar(C3[:, 4:5], C3[:, 1:2], -1.0, None, ALU.mult)
            nc.vector.tensor_scalar(C3[:, 3:4], C3[:, 3:4], -0.8, None, ALU.mult).then_inc(guard3, 1)
            dve.wait_ge(v3_exp, 1)
            link(nc.vector.tensor_tensor(WH[:, :, 0:W2], WH[:, :, 0:W2], V3[:, :].unsqueeze(2).to_broadcast([P, T, W2]), ALU.mult))
            dve.wait_ge(r3_exp, 1)
            for t in range(T):
                nc.vector.scalar_tensor_tensor(Z[:, t, :], R3[:, :], S3[:, t:t + 1], AT[:, t, 0:N], ALU.max, ALU.mult).then_inc(p3_ready, 1)
            dve.wait_ge(num3_mm, 1)
            nc.vector.reciprocal(RDEN[:, 0:TA], VA[:, :, D])
            link(nc.vector.reciprocal(RDEN[:, TA:T], VB[:, :, D]))
            nc.vector.tensor_tensor(NRM[:, 0:TA, :], VA[:, :, 0:D], wide(RDEN[:, 0:TA], TA), ALU.mult)
            link(nc.vector.tensor_tensor(NRM[:, TA:T, :], VB[:, :, 0:D], wide(RDEN[:, TA:T], T - TA), ALU.mult))
            nc.vector.tensor_scalar(CEN[:, :, :], NRM[:, :, :], 0.0, None, ALU.min).then_inc(elu_in, 1)
            link(nc.vector.tensor_scalar(RES[:, :, :], NRM[:, :, :], 0.0, None, ALU.max))
            dve.wait_ge(elu_exp, 1)
            link(nc.vector.scalar_tensor_tensor(NRM[:, :, :], SQ[:, :, :], -1.0, RES[:, :, :], ALU.add, ALU.add))
            link(nc.vector.tensor_tensor(NRM[:, :, :], NRM[:, :, :], X[3][:, :, :], ALU.add))
            layer_norm(NRM, Y, 0, T).then_inc(x_ready, 1)

        @block.tensor
        def _(pe):
            mm, tr = nc.tensor.matmul, nc.tensor.transpose

            pe.wait_ge(idents, 3)
            pe.wait_ge(x_in, 32)
            for t in range(T):
                ins = tr(PSflat[0:D, t * P:(t + 1) * P], X[0][:, t, :], IDF[:, :])
            ins.then_inc(x0t_mm, 1)
            pe.wait_ge(x0t_sb, 1)
            pe.wait_ge(wb_in, 3 * 16)
            pe.wait_ge(consts, 1)
            for t in range(T):
                mm(PSflat[:, 3 * 512 + t * D:3 * 512 + (t + 1) * D], XT[:, t * P:(t + 1) * P], FC1[:, :], start=True, stop=True)
            pe.wait_ge(x1_rows, 1)
            mm(PS[:, 5, 0:D], X1R[:, :], FC2[:, :], start=True, stop=True).then_inc(hid_mm, 1)

            def adj_transposed(it):
                pe.wait_ge(an_ready, it + 1)
                for j in range(T):
                    ins = tr(PSTR[:, j * P:(j + 1) * P], AN[:, bass.ds(it, 1), j * P:(j + 1) * P].rearrange("p a j -> p (a j)"), IDB[:, :])
                ins.then_inc(at_mm, 1)

            def sums(it, width, signal):
                xs = XS[0] if width == W0 else XS[1]
                for j in range(T):
                    ins = mm(PSN[:, bass.ds(it, 1), 0:width].rearrange("p a n -> p (a n)"),
                             AT[:, j, bass.ds(it * P, P)], xs[:, j, 0:width], start=j == 0, stop=j == T - 1)
                ins.then_inc(signal, 1)

            pe.wait_ge(xs_ready, 1)
            pe.wait_ge(consts, 2)
            adj_transposed(0)
            with pe.Fori(0, T // 2) as pair:
                for it in (2 * pair + 1, 2 * pair + 2):
                    pe.wait_ge(at_lo, it)
                    pe.wait_ge(at_hi, it)
                    adj_transposed(it)
                    pe.wait_ge(score_dif, 1)
                    sums(it - 1, W0, sum0_mm)
            pe.wait_ge(at_lo, T)
            pe.wait_ge(at_hi, T)
            sums(T - 1, W0, sum0_mm)

            pe.wait_ge(w_in, 12 * 16)
            pe.wait_ge(x_ready, 2)
            for c in range(4):
                tr(PS[:, 6, c * W2:(c + 1) * W2], QS[:, c * P:(c + 1) * P], IDF[0:W2, 0:W2])
                tr(PS[:, 7, c * W2:(c + 1) * W2], KS[:, c * P:(c + 1) * P], IDF[0:W2, 0:W2])
            for h in range(H):
                tr(PS[0:D, h // 4, h % 4 * W2:(h % 4 + 1) * W2], VS[:, h * D:(h + 1) * D], IDF[0:W2, 0:W2])
            tr(PS[0:D, 2, 0:D], W3S[0:D, 0:D], IDF[0:D, 0:D]).then_inc(wts_mm, 1)
            pe.wait_ge(wts_sb, 1)
            for half in range(2):
                for c in range(4):
                    mm(PS[0:W2, 3, half * 2 * H:(half + 1) * 2 * H], QKT[:, 4 * half + c, :],
                       AW[:, 4 * half + c, :, :].rearrange("p k h -> p (k h)"), start=c == 0, stop=c == 3)
            mm(PS[0:D, 3, 64:66], WT[:, :], A3[:, :], start=True, stop=True)
            for h in range(H):
                ins = mm(PS[0:W2, 6, h * D:(h + 1) * D], VWT[:, h, :], PWS[:, h, :], start=True, stop=True)
            ins.then_inc(fold_mm, 1)

            pe.wait_ge(fold_sb, 1)
            pe.wait_ge(x_ready, len(GROUPS))
            with pe.Fori(0, 2) as group:
                for u in range(4):
                    sums(4 * group + u, 3 * D, sum1_mm)
            for t in range(8, T):
                sums(t, 3 * D, sum1_mm)

            def x_transposed(layer, src, after):
                for n, (lo, hi) in enumerate(GROUPS):
                    pe.wait_ge(x_ready, len(GROUPS) * (layer + 1) + n + 1)
                    if n == 2:
                        pe.wait_ge(xt_sb, len(GROUPS) * layer + 1)
                    for t in range(lo, hi):
                        ins = tr(PS[0:D, 6 + n % 2, (t - lo) * P:(t - lo + 1) * P], src[:, t, :], IDF[:, :])
                    ins.then_inc(xt_mm, 1)
                    pe.wait_ge(xt_sb, len(GROUPS) * layer + n + 1)
                    after(n, *CHUNKS[n])

            def row(h, half):
                for c in range(0, HALF, 512):
                    w = min(512, HALF - c)
                    ins = mm(MISC[:, c:c + w], PICK0[:, bass.ds(h, 1), :].rearrange("p a n -> p (a n)"),
                             TERMS[:, half * HALF + c:half * HALF + c + w], start=True, stop=True)
                ins.then_inc(row_mm, 1)

            def values(h, lo, hi):
                for t in range(lo, hi):
                    ins = mm(v_block(t), XT[:, t * P:(t + 1) * P], VP[:, bass.ds(h, 1), :].rearrange("p a n -> p (a n)"), start=True, stop=True)
                if hi == T:
                    ins.then_inc(val_mm, 1)

            pe.wait_ge(consts, 5)
            pe.wait_ge(terms_set, 2)
            pe.wait_ge(lhs_set, H)
            x_transposed(0, X[2], lambda n, c, w: mm(PSflat[0:4 * H, c:c + w], W32[:, :], XT[:, c:c + w], start=True, stop=True).then_inc(ab_mm, 1))
            for t in range(T):
                ins = mm(PS[:, 3, 64 + t * H:64 + (t + 1) * H], XT[:, t * P:(t + 1) * P], W32[:, 2 * H:3 * H], start=True, stop=True)
            ins.then_inc(b0_mm, 1)
            values(0, 0, T)
            pe.wait_ge(mxr_ready, 1)
            mm(PS[:, 4, 0:4 * H], MXR[:, :], IDF[0:4 * H, 0:4 * H], start=True, stop=True).then_inc(max_mm, 1)

            def z1(h, t):
                for c, w in CHUNKS:
                    ins = mm(ZP[:, c:c + w], LHS1[:, bass.ds(h, 1), t * P:(t + 1) * P].rearrange("p a n -> p (a n)"),
                             TERMS[:, c:c + w], start=True, stop=True)
                ins.then_inc(z1_mm, 1)

            def weigh(h, t, par, first):
                k = rows_of(t)
                if t == 0:
                    pe.wait_ge(val_sb, h + 1)
                pe.wait_ge(p_ready, h * T + t + 1)
                for n, (c, w) in enumerate(CHUNKS):
                    if t == 0 and not first:
                        pe.wait_ge(acc_sb, 3 * (h - 1) + n + 1)
                    ins = mm(ACC[0:W2, c:c + w], VST[par][0:k, t, :], Z[0:k, t, c:c + w], start=t == 0, stop=t == T - 1)
                    if t == T - 1:
                        ins.then_inc(acc_mm, 1)
                    if n == len(CHUNKS) - 1 and t < T - 1:
                        ins.then_inc(p_used, 1)
                if t == T - 1:
                    pe.sem_inc(p_used, 1)

            def sums_back(h):
                pe.wait_ge(acc_sb, 3 * h + 3)
                for t in range(T):
                    ins = tr(v_block(t), NUMT[:, t * P:(t + 1) * P], IDF[0:W2, 0:W2])
                ins.then_inc(num_mm, 1)

            def head(h, par, first, last):
                for t in range(T):
                    pe.wait_ge(z_ready, h * T + t + 1)
                    if t < T - 1:
                        z1(h, t + 1)
                    elif not last:
                        z1(h + 1, 0)
                    if t >= 3:
                        weigh(h, t - 3, par, first)
                    elif not first:
                        weigh(h - 1, T - 3 + t, 1 - par, False)
                    if t == 4 and not first:
                        pe.wait_ge(val_sb, h + 1)
                        sums_back(h - 1)
                    if not last:
                        if t == 6:
                            if not first:
                                pe.wait_ge(norm_step, 2 * h)
                            row(h + 1, 0)
                        if t == 7:
                            pe.wait_ge(row_sb, 2 * (h + 1) + 1)
                            row(h + 1, 1)
                        if t == 8:
                            pe.wait_ge(row_sb, 2 * (h + 1) + 2)
                        if t >= 8:
                            values(h + 1, 4 * (t - 8), min(4 * (t - 7), T))

            pe.wait_ge(mid_ready, len(CHUNKS))
            pe.wait_ge(lo_ready, len(CHUNKS))
            pe.wait_ge(val_sb, 1)
            row(0, 0)
            pe.wait_ge(row_sb, 1)
            row(0, 1)
            pe.wait_ge(guards, 1)
            pe.wait_ge(b1_in, 3 * len(CHUNKS) * 16)
            z1(0, 0)
            head(0, 0, True, False)
            with pe.Fori(0, H // 2 - 1) as pair:
                head(2 * pair + 1, 1, False, False)
                head(2 * pair + 2, 0, False, False)
            head(H - 1, 1, False, True)
            for t in range(T - 3, T):
                weigh(H - 1, t, 1, False)
            sums_back(H - 1)

            def group3(n, c, w):
                for t in range(*GROUPS[n]):
                    ins = mm(wh_block(t), XT[:, t * P:(t + 1) * P], W3S[:, :], start=True, stop=True)
                if n == len(GROUPS) - 1:
                    ins.then_inc(wh_mm, 1)
                ins = mm(ACC[:, c:c + w], FREP[:, :], XT[0:D, c:c + w], start=True, stop=True)
                if n == len(GROUPS) - 1:
                    ins.then_inc(f_mm, 1)
            pe.wait_ge(acc_sb, 3 * H)
            pe.wait_ge(norm_step, 2 * H)
            pe.wait_ge(f_rows, 1)
            x_transposed(1, X[3], group3)
            pe.wait_ge(wh_sb, 1)
            pe.wait_ge(max3_ready, 1)
            tr(PS[0:3, 6, 0:P], MX3[:, :], IDF[:, :]).then_inc(max3_mm, 1)
            pe.wait_ge(max3_ready, 2)
            mm(PS[:, 6, 0:3], MX3T[:, 0:P], IDF[0:3, 0:3], start=True, stop=True).then_inc(max3_mm, 1)
            for t in range(T):
                k = rows_of(t)
                pe.wait_ge(p3_ready, t + 1)
                for c, w in CHUNKS:
                    ins = mm(ZP[0:W2, c:c + w], WH[0:k, t, 0:W2], Z[0:k, t, c:c + w], start=t == 0, stop=t == T - 1)
                    if t == T - 1:
                        ins.then_inc(acc3_mm, 1)
            pe.wait_ge(acc3_sb, len(CHUNKS))
            for t in range(T):
                ins = tr(v_block(t), NUMT[:, t * P:(t + 1) * P], IDF[0:W2, 0:W2])
            ins.then_inc(num3_mm, 1)


_INS = ['x', 'adj', 'L0_gnn_fc_w', 'L0_gnn_fc_b', 'L0_gnn_attn_w', 'L0_gnn_attn_b', 'L2_gnn_Qw', 'L2_gnn_Qb',
        'L2_gnn_Kw', 'L2_gnn_Kb', 'L2_gnn_Vw', 'L2_gnn_Vb', 'L2_gnn_a', 'L2_gnn_Pw', 'L2_gnn_Pb', 'L3_gnn_W', 'L3_gnn_a']


def kernel(**inputs):
    import concourse.bacc as _bacc
    from concourse.bass_utils import run_bass_kernel_spmd as _run

    nc = _bacc.Bacc("TRN2", target_bir_lowering=False, num_devices=1)
    arrays, args = {}, []
    for name in _INS:
        arr = np.ascontiguousarray(inputs[name])
        arrays[f"in_{name}_dram"] = arr
        args.append(nc.dram_tensor(f"in_{name}_dram", arr.shape, mybir.dt.from_np(arr.dtype), kind="ExternalInput").ap())
    args.append(nc.dram_tensor("out_dram", (N, D), F32, kind="ExternalOutput").ap())
    graph_kernel(nc, *args)
    r = _run(nc, [arrays], core_ids=[0])
    return r.results[0]["out_dram"]
```

```python
from contextlib import ExitStack

import numpy as np
import concourse.bass as bass
from concourse import mybir
from concourse.alu_op_type import AluOpType as ALU

ACT = mybir.ActivationFunctionType
F32 = mybir.dt.float32
BF16 = mybir.dt.bfloat16
I32 = mybir.dt.int32
U16 = mybir.dt.uint16
X_AXIS = mybir.AxisListType.X

P = 128
N, D = 1354, 64
T = -(-N // P)
NP = T * P
LAST = N - (T - 1) * P
H = 8
DH = H * D
EPS = 1e-5
CHUNKS = [(c, min(512, N - c)) for c in range(0, N, 512)]
PADDED = [(c, min(512, NP - c)) for c in range(0, NP, 512)]
HALF = N // 2
GROUPS = [(0, 4), (4, 8), (8, T)]
NORM_STEPS = 8
SKEW = (0, 6, 9)
SKEW1 = 6
W0 = 3 * D + 1
W2 = D + 1
W3 = D + 3
B1_FIRST = 1024
STEPS = 5
STAGES = 5
TA = 7


def rows_of(t):
    return LAST if t == T - 1 else P


def graph_kernel(nc, x, adj, fc_w, fc_b, attn_w, attn_b, Qw, Qb, Kw, Kb, Vw, Vb, a, Pw, Pb, W, a3, out, a0_rows):
    with ExitStack() as ctx:
        def sb(name, shape, dt=F32):
            return ctx.enter_context(nc.sbuf_tensor(name, shape, dt))

        def sem(name):
            return ctx.enter_context(nc.semaphore(name))

        AT = sb("AT", [P, T, NP], BF16)
        Z = sb("Z", [P, T, N])
        Zflat = Z[:, :, :].rearrange("p t n -> p (t n)")
        AN_WORDS = T * NP // 2
        AN = Zflat[:, 0:AN_WORDS].bitcast(BF16).rearrange("p (t n) -> p t n", t=T)
        STAGE = Zflat[:, AN_WORDS:AN_WORDS + STAGES * N].bitcast(I32).rearrange("p (s n) -> p s n", s=STAGES)
        X = [sb(f"X{i}", [P, T, D]) for i in range(3)]
        X.append(X[0])
        XS = [sb(f"XS{i}", [P, T, W0], BF16) for i in range(2)]
        RES = sb("RES", [P, T, D])
        Y = sb("Y", [P, T, D])
        CEN = sb("CEN", [P, T, D])
        SQ = sb("SQ", [P, T, D])
        STAT = sb("STAT", [P, 8, T])
        XT = sb("XT", [W2, NP])
        NUMT = sb("NUMT", [W2, NP])
        TERMS = sb("TERMS", [P, N], BF16)
        PICK0 = sb("PICK0", [P, P], BF16)
        LHS1 = sb("LHS1", [P, H, NP], BF16)
        SEL = sb("SEL", [P, 2, H], BF16)
        SELF = sb("SELF", [P, 2, H])
        ROW0 = [sb(f"ROW0_{i}", [P, N]) for i in range(2)]
        VST = [sb(f"VST{i}", [P, T, W2]) for i in range(2)]
        B0 = sb("B0", [P, T, H])
        NEGC = sb("NEGC", [P, H])
        AB = Z[0:4 * H, T - 1, :]
        R1 = Z[0:4 * H, T - 2, :]
        MID = Z[0:4 * H, T - 3, :].bitcast(BF16)[:, 0:N]
        WH = sb("WH", [P, T, W3])
        BACK = WH[:, :, 0:W2]
        IDF = sb("IDF", [P, P])
        IDB = sb("IDB", [P, P], BF16)
        ONES = sb("ONES", [P, P])
        QS, KS = ROW0[0][0:W2, 0:DH], ROW0[0][0:W2, DH:2 * DH]
        VS = ROW0[1][0:W2, 0:DH]
        QKT = ROW0[1][:, DH:DH + 8 * W2].rearrange("p (c d) -> p c d", d=W2)
        VWT = VST[0][0:D, 0:H, :]
        PWS = VST[1][0:D, 0:H, 0:D]
        AW = sb("AW", [P, 8, 2, H])
        W32 = sb("W32", [W2, 4 * H])
        VP = sb("VP", [W2, DH])
        VALL = sb("VALL", [P, T, DH])
        W3S = sb("W3S", [W2, W3])
        A3 = sb("A3", [D, 2])
        WT = sb("WT", [D, D])
        WA3 = sb("WA3", [D, 2])
        FREP = sb("FREP", [D, P])
        FC1 = sb("FC1", [W2, D])
        FC2 = sb("FC2", [D, D])
        X1R = sb("X1R", [D, P])
        NEIGH = sb("NEIGH", [P, D])
        ATW = sb("ATW", [P, D])
        ATB = sb("ATB", [P, 1])
        PBB = sb("PBB", [P, D])
        SC = sb("SC", [P, 3, T])
        WROW = sb("WROW", [P, T])
        MX = sb("MX", [4 * H, 1])
        MXR = sb("MXR", [4 * H, P])
        G2 = sb("G2", [P, 3, 2 * H])
        RDEN = sb("RDEN", [P, T])
        NRM = sb("NRM", [P, T, D])
        MX3 = sb("MX3", [P, 3])
        MX3T = sb("MX3T", [2, P + 1])
        NEG3 = sb("NEG3", [P, 2])
        C3 = sb("C3", [P, 2])
        R3 = ROW0[0]
        S3 = sb("S3", [P, T])
        V3 = sb("V3", [P, T])

        PS = ctx.enter_context(nc.psum_tensor("PS", [P, 8, 512], F32))
        PSflat = PS[:, :, :].rearrange("p b n -> p (b n)")
        PSN = PSflat[:, 0:3072].rearrange("p (t n) -> p t n", n=256)
        PSTR = PSflat[:, 3072:4096].bitcast(BF16)
        AT_LO = PSTR[:, 0:8 * P].rearrange("p (j i) -> p j i", i=P)
        AT_HI = PSTR[:, 8 * P:T * P].rearrange("p (j i) -> p j i", i=P)
        ACC = PSflat[:, 0:N]
        ZP = PSflat[:, 1536:1536 + N]
        MISC = PSflat[:, 3072:4096]

        def two_banks(bank, width):
            return (PS[:, bank, 0:TA * width].rearrange("p (t n) -> p t n", n=width),
                    PS[:, bank + 1, 0:(T - TA) * width].rearrange("p (t n) -> p t n", n=width),
                    lambda t: PS[:, bank + t // TA, t % TA * width:t % TA * width + width])

        VA, VB, v_block = two_banks(6, W2)

        def vall_bank(t):
            return 1 if t == 0 else 6 + t % 2

        def group_bank(bank, n, width):
            tiles = GROUPS[n][1] - GROUPS[n][0]
            return PS[:, bank + n, 0:tiles * width].rearrange("p (t n) -> p t n", n=width)


        x_in, w_in, wb_in = sem("x_in"), sem("w_in"), sem("wb_in")
        adj_in = [sem(f"adj_in{t}") for t in range(T)]
        w3_zero = sem("w3_zero")
        consts, x_pad, idents, an_pads = sem("consts"), sem("x_pad"), sem("idents"), sem("an_pads")
        terms_set, sel_step, lhs_set = sem("terms_set"), sem("sel_step"), sem("lhs_set")
        b1_in = [sem("b1_in_first"), sem("b1_in_rest")]
        hi_ready, mid_ready, lo_ready, r1_ready = sem("hi_ready"), sem("mid_ready"), sem("lo_ready"), sem("r1_ready")
        x0t_mm, x0t_sb, wts_mm, wts_sb = sem("x0t_mm"), sem("x0t_sb"), sem("wts_mm"), sem("wts_sb")
        fold_mm, fold_sb, hid_mm, hid_read = sem("fold_mm"), sem("fold_sb"), sem("hid_mm"), sem("hid_read")
        score_dif, score_exp = sem("score_dif"), sem("score_exp")
        xs_ready, an_ready, at_mm, at_lo, at_hi = sem("xs_ready"), sem("an_ready"), sem("at_mm"), sem("at_lo"), sem("at_hi")
        sum0_mm, sum1_mm = sem("sum0_mm"), sem("sum1_mm")
        var_ready, rstd_ready, x_ready = sem("var_ready"), sem("rstd_ready"), sem("x_ready")
        xt_mm, xt_sb = sem("xt_mm"), sem("xt_sb")
        ab_mm = sem("ab_mm")
        b0_mm, b0_sb, mxr_ready, max_mm, guards = sem("b0_mm"), sem("b0_sb"), sem("mxr_ready"), sem("max_mm"), sem("guards")
        a0_out, row_in, row_mm, row_sb = sem("a0_out"), sem("row_in"), sem("row_mm"), sem("row_sb")
        val_mm, vall_sb, v0_set, val_sb = sem("val_mm"), sem("vall_sb"), sem("v0_set"), sem("val_sb")
        val_ones, back_sb, rden_ready = sem("val_ones"), sem("back_sb"), sem("rden_ready")
        num_scaled, last_mm = sem("num_scaled"), sem("last_mm")
        tiles_picked = sem("tiles_picked")
        z0_ready, z1_mm, z_ready = sem("z0_ready"), sem("z1_mm"), sem("z_ready")
        leaky_ready, p_ready, p_used = sem("leaky_ready"), sem("p_ready"), sem("p_used")
        acc_mm, acc_sb, num_mm, num_added = sem("acc_mm"), sem("acc_sb"), sem("num_mm"), sem("num_added")
        wh_mm, wh_sb, guard3 = sem("wh_mm"), sem("wh_sb"), sem("guard3")
        f_rows, f_mm, max3_ready, max3_mm = sem("f_rows"), sem("f_mm"), sem("max3_ready"), sem("max3_mm")
        v3_exp, r3_exp, pb_in, atw_in, x1_rows = sem("v3_exp"), sem("r3_exp"), sem("pb_in"), sem("atw_in"), sem("x1_rows")
        waits_done = sem("waits_done")
        p3_ready, acc3_mm, acc3_sb, num3_mm = sem("p3_ready"), sem("acc3_mm"), sem("acc3_sb"), sem("num3_mm")
        elu_in, elu_exp, out_done = sem("elu_in"), sem("elu_exp"), sem("out_done")

        block = ctx.enter_context(nc.Block())

        @block.sync
        def _(sp):
            sp.wait_ge(x_pad, 1)
            sp.dma_start(X[0][:, 0:T - 1, :], x[0:(T - 1) * P, :].rearrange("(t p) d -> p t d", p=P)).then_inc(x_in, 16)
            sp.dma_start(X[0][0:LAST, T - 1, :], x[(T - 1) * P:N, :]).then_inc(x_in, 16)
            for t in range(T):
                if t >= STAGES:
                    sp.wait_ge(an_ready, t - STAGES + 1)
                sp.dma_start(STAGE[0:rows_of(t), t % STAGES, :], adj[t * P:t * P + rows_of(t), :]).then_inc(adj_in[t], 16)
            sp.wait_ge(lhs_set, H)
            for part, chunks, lo, hi in ((0, 2, 0, B1_FIRST), (1, len(CHUNKS), B1_FIRST, N)):
                for s, ready in enumerate((hi_ready, mid_ready, lo_ready)):
                    sp.wait_ge(ready, chunks)
                    sp.dma_start(LHS1[96 + s:97 + s, :, lo:hi], TERMS[32 * s + 3 * H:32 * s + 4 * H, lo:hi]).then_inc(b1_in[part], 16)
            sp.wait_ge(hi_ready, len(CHUNKS))
            sp.dma_start(a0_rows[:, :], AB[0:H, :]).then_inc(a0_out, 16)
            sp.wait_ge(a0_out, 16)
            for h in range(1, H):
                if h >= 2:
                    sp.wait_ge(row_in, 16 * (h - 1))
                    sp.wait_ge(z0_ready, (h - 1) * T)
                sp.dma_start(ROW0[h % 2][:, :], a0_rows[h, :].partition_broadcast(P)).then_inc(row_in, 16)
            for n, (lo, hi) in enumerate(GROUPS):
                whole = min(hi, T - 1)
                sp.wait_ge(x_ready, 3 * len(GROUPS) + n + 1)
                sp.dma_start(out[lo * P:whole * P, :].rearrange("(t p) d -> p t d", p=P), Y[:, lo:whole, :]).then_inc(out_done, 16)
            sp.dma_start(out[(T - 1) * P:N, :], Y[0:LAST, T - 1, :]).then_inc(out_done, 16)
            sp.wait_ge(out_done, (len(GROUPS) + 1) * 16)

        @block.gpsimd
        def _(pool):
            count = {}

            def alone(ins, signal):
                count[signal.name] = count.get(signal.name, 0) + 1
                ins.then_inc(signal, 1)
                pool.wait_ge(signal, count[signal.name])

            alone(nc.gpsimd.memset(X[0][:, T - 1, :], 0.0), x_pad)
            alone(nc.gpsimd.memset(ONES[:, :], 1.0), idents)
            alone(nc.gpsimd.affine_select(out=IDF[:, :], in_=ONES[:, :], compare_op=ALU.is_equal, fill=0.0, base=0,
                                          pattern=[[-1, P]], channel_multiplier=1), idents)
            alone(nc.gpsimd.tensor_copy(IDB[:, :], IDF[:, :]), idents)
            alone(nc.gpsimd.memset(XT[D:W2, :], 1.0), consts)
            alone(nc.gpsimd.memset(XS[0][:, :, W0 - 1:W0], 1.0), consts)
            alone(nc.gpsimd.memset(AN[:, :, N:NP], 0.0), an_pads)
            alone(nc.gpsimd.memset(AN[:, T - 1, 0:N], 1.0), an_pads)
            for k in range(2):
                hi, mid, lo = (IDF[:, q + k * H:q + (k + 1) * H] for q in (0, 32, 64))
                alone(nc.gpsimd.tensor_tensor(SELF[:, k, :], hi, mid, ALU.add), sel_step)
                alone(nc.gpsimd.tensor_tensor(SEL[:, k, :], SELF[:, k, :], lo, ALU.add), sel_step)
            for dst, weight, bias in ((QS, Qw, Qb), (KS, Kw, Kb), (VS, Vw, Vb)):
                pool.dma_start(dst[0:D, :], weight).then_inc(w_in, 16)
                pool.dma_start(dst[D:W2, :], bias.unsqueeze(0)).then_inc(w_in, 16)
            pool.dma_start(PWS[:, :, :], Pw.rearrange("(h d) o -> d h o", d=D)).then_inc(w_in, 16)
            pool.dma_start(A3[:, 0:1], a3[0:D, :]).then_inc(w_in, 16)
            pool.dma_start(A3[:, 1:2], a3[D:2 * D, :]).then_inc(w_in, 16)
            for k in range(2):
                pool.dma_start(AW[:, :, k, :], a[k].rearrange("(c p) h -> p c h", p=P)).then_inc(w_in, 16)
            pool.dma_start(PBB[:, :], Pb.partition_broadcast(P)).then_inc(pb_in, 16)
            alone(nc.gpsimd.memset(W3S[:, :], 0.0), w3_zero)
            pool.dma_start(W3S[0:D, 0:D], W).then_inc(w_in, 16)
            alone(nc.gpsimd.memset(W3S[D:W2, D:D + 1], 1.0), consts)
            alone(nc.gpsimd.memset(TERMS[96:P, :], 1.0), terms_set)
            alone(nc.gpsimd.tensor_copy(PICK0[:, :], SEL[:, 0, 0:1].to_broadcast([P, P])), terms_set)
            for n in range(4 * len(GROUPS)):
                if n == len(GROUPS):
                    pool.wait_ge(fold_mm, 1)
                    for values in VST:
                        alone(nc.gpsimd.memset(values[:, :, D:W2], 1.0), val_ones)
                if n == 2 * len(GROUPS):
                    pool.wait_ge(x_ready, n)
                    pool.wait_ge(pb_in, 16)
                    alone(nc.gpsimd.tensor_tensor(Y[:, :, :], X[2][:, :, :], PBB[:, :].unsqueeze(1).to_broadcast([P, T, D]), ALU.add), num_added)
                    for t in range(T):
                        pool.wait_ge(vall_sb, t + 1)
                        alone(nc.gpsimd.tensor_copy(VST[0][:, t, 0:D], VALL[:, t, 0:D]), v0_set)
                    for h in range(H - 1):
                        pool.wait_ge(rden_ready, h + 1)
                        alone(nc.gpsimd.tensor_tensor(BACK[:, :, 0:D], BACK[:, :, 0:D],
                                                      RDEN[:, :].unsqueeze(2).to_broadcast([P, T, D]), ALU.mult), num_scaled)
                        alone(nc.gpsimd.tensor_tensor(Y[:, :, :], Y[:, :, :], BACK[:, :, 0:D], ALU.add), num_added)
                lo, hi = GROUPS[n % len(GROUPS)]
                pool.wait_ge(var_ready, n + 1)
                alone(nc.gpsimd.tensor_tensor(STAT[:, 3, lo:hi], STAT[:, 2, lo:hi], STAT[:, 7, lo:hi], ALU.pow), rstd_ready)

        @block.scalar
        def _(act):
            act.dma_start(FC1[0:D, :], fc_w[0:D, :]).then_inc(wb_in, 16)
            act.dma_start(FC1[D:W2, :], fc_b.unsqueeze(0)).then_inc(wb_in, 16)
            act.dma_start(FC2[:, :], fc_w[D:2 * D, :]).then_inc(wb_in, 16)
            act.dma_start(ATW[:, :], attn_w.rearrange("d o -> (d o)").partition_broadcast(P)).then_inc(atw_in, 16)
            act.dma_start(ATB[:, :], attn_b.partition_broadcast(P)).then_inc(atw_in, 16)
            act.wait_ge(x0t_mm, 1)
            nc.scalar.activation(XT[0:D, :], PSflat[0:D, 0:NP], ACT.Copy).then_inc(x0t_sb, 1)

            act.wait_ge(an_pads, 2)
            for t in range(T):
                if t == 4:
                    act.wait_ge(score_dif, 1)
                    nc.scalar.activation(WROW[:, :], SC[:, 2, :], ACT.Exp).then_inc(score_exp, 1)
                act.wait_ge(adj_in[t], 16)
                nc.scalar.activation(AN[0:rows_of(t), t, 0:N], STAGE[0:rows_of(t), t % STAGES, :], ACT.Copy).then_inc(an_ready, 1)
                if t >= 1:
                    act.wait_ge(at_mm, t)
                    nc.scalar.activation(AT[:, 8:T, (t - 1) * P:t * P], AT_HI, ACT.Copy).then_inc(at_hi, 1)
            act.wait_ge(at_mm, T)
            nc.scalar.activation(AT[:, 8:T, (T - 1) * P:NP], AT_HI, ACT.Copy).then_inc(at_hi, 1)

            act.wait_ge(wts_mm, 1)
            nc.scalar.activation(QKT[:, 0:4, :], PS[:, 6, 0:4 * W2].rearrange("p (c d) -> p c d", d=W2), ACT.Copy)
            nc.scalar.activation(QKT[:, 4:8, :], PS[:, 7, 0:4 * W2].rearrange("p (c d) -> p c d", d=W2), ACT.Copy)
            nc.scalar.activation(WT[:, :], PS[0:D, 2, 0:D], ACT.Copy)
            for half in range(2):
                ins = nc.scalar.activation(VWT[:, 4 * half:4 * half + 4, :], PS[0:D, half, 0:4 * W2].rearrange("p (h d) -> p h d", d=W2), ACT.Copy)
            ins.then_inc(wts_sb, 1)
            act.wait_ge(fold_mm, 1)
            nc.scalar.activation(W32[:, :], PS[0:W2, 3, 0:4 * H], ACT.Copy)
            nc.scalar.activation(W3S[0:D, D + 1:D + 2], PS[0:D, 3, 65:66], ACT.Copy)
            nc.scalar.activation(W3S[0:D, D + 2:D + 3], PS[0:D, 3, 64:65], ACT.Copy)
            nc.scalar.activation(WA3[:, :], PS[0:D, 3, 64:66], ACT.Copy)
            nc.scalar.activation(VP[:, :], PS[0:W2, 6, :], ACT.Copy).then_inc(fold_sb, 1)

            act.wait_ge(sel_step, 4)
            for h in range(H):
                nc.scalar.activation(LHS1[:, h, :], SEL[:, 1, h:h + 1].to_broadcast([P, NP]), ACT.Copy).then_inc(lhs_set, 1)

            def xt_copy(layer, n):
                lo, hi = GROUPS[n]
                act.wait_ge(xt_mm, layer * len(GROUPS) + n + 1)
                nc.scalar.activation(XT[0:D, lo * P:hi * P], PS[0:D, 6 + n % 2, 0:(hi - lo) * P], ACT.Copy).then_inc(xt_sb, 1)

            def vall_copy(lo, hi):
                for t in range(lo, hi):
                    act.wait_ge(val_mm, t + 1)
                    nc.scalar.activation(VALL[:, t, :], PS[:, vall_bank(t), :], ACT.Copy).then_inc(vall_sb, 1)

            def ab_copy(n):
                c, w = CHUNKS[n]
                act.wait_ge(ab_mm, n + 1)
                nc.scalar.activation(AB[:, c:c + w], PS[0:4 * H, 0, 0:w], ACT.Copy)
                nc.scalar.activation(TERMS[0:32, c:c + w], PS[0:4 * H, 0, 0:w], ACT.Copy).then_inc(hi_ready, 1)

            def mid_copy(n):
                c, w = CHUNKS[n]
                act.wait_ge(r1_ready, n + 1)
                nc.scalar.activation(TERMS[32:64, c:c + w], R1[:, c:c + w], ACT.Copy).then_inc(mid_ready, 1)

            def row_copy(half, src):
                act.wait_ge(row_mm, half + 1)
                nc.scalar.activation(ROW0[0][:, half * HALF:(half + 1) * HALF], src[:, 0:HALF], ACT.Copy).then_inc(row_sb, 1)

            def back_copy(h):
                act.wait_ge(num_mm, h + 1)
                act.wait_ge(num_added, h + 1)
                nc.scalar.activation(BACK[:, 0:TA, :], VA, ACT.Copy)
                nc.scalar.activation(BACK[:, TA:T, :], VB, ACT.Copy).then_inc(back_sb, 1)

            def val_copy(h, par):
                nc.scalar.activation(VST[par][:, :, 0:D], VALL[:, :, bass.ds(h * D, D)], ACT.Copy).then_inc(val_sb, 1)

            def z0(h, t, par, reused):
                if t == 0 and reused:
                    act.wait_ge(row_in, 16 * h)
                if reused:
                    act.wait_ge(p_used, (h - 1) * T + t + 1)
                act.sem_inc(waits_done, 1)
                nc.scalar.activation(Z[:, t, :], ROW0[par][:, :], ACT.Identity, bias=B0[:, t, bass.ds(h, 1)]).then_inc(z0_ready, 1)

            def exp(h, t):
                act.wait_ge(leaky_ready, h * T + t + 1)
                act.sem_inc(waits_done, 1)
                nc.scalar.activation(Z[:, t, :], Z[:, t, :], ACT.Exp, bias=NEGC[:, bass.ds(h, 1)]).then_inc(p_ready, 1)

            def sums_copy(h):
                for n, (c, w) in enumerate(CHUNKS):
                    act.wait_ge(acc_mm, 3 * h + n + 1)
                    nc.scalar.activation(NUMT[:, c:c + w], ACC[0:W2, c:c + w], ACT.Copy).then_inc(acc_sb, 1)

            def head(h, par, first, last):
                for t in range(T):
                    if first and t == T - 2:
                        act.wait_ge(a0_out, 16)
                    if t < T - 1:
                        z0(h, t + 1, par, not first)
                    elif not last:
                        z0(h + 1, 0, 1 - par, True)
                    if t == 3 and not first:
                        sums_copy(h - 1)
                    if t >= 2:
                        exp(h, t - 2)
                    elif not first:
                        exp(h - 1, T - 2 + t)
                    if t == 1 and not first:
                        val_copy(h, par)
                    if first and t < T - 2:
                        vall_copy(t + 2, t + 3)
                    if first and t == 0:
                        act.wait_ge(guards, 1)
                    if t == 5 and not first:
                        back_copy(h - 1)

            xt_copy(0, 0)
            ab_copy(0)
            vall_copy(0, 1)
            xt_copy(0, 1)
            ab_copy(1)
            xt_copy(0, 2)
            mid_copy(0)
            mid_copy(1)
            ab_copy(2)
            mid_copy(2)
            row_copy(0, MISC)
            row_copy(1, PSflat[:, 512:])
            act.wait_ge(row_sb, 2)
            act.wait_ge(b0_sb, 1)
            z0(0, 0, 0, False)
            vall_copy(1, 2)
            act.wait_ge(val_ones, len(VST))
            head(0, 0, True, False)
            with act.Fori(0, H // 2 - 1) as pair:
                head(2 * pair + 1, 1, False, False)
                head(2 * pair + 2, 0, False, False)
            head(H - 1, 1, False, True)
            exp(H - 1, T - 2)
            exp(H - 1, T - 1)
            sums_copy(H - 1)

            def wh_copy(n):
                lo, hi = GROUPS[n]
                act.wait_ge(wh_mm, n + 1)
                nc.scalar.activation(WH[:, lo:hi, :], group_bank(3, n, W3), ACT.Copy).then_inc(wh_sb, 1)

            xt_copy(1, 0)
            wh_copy(0)
            xt_copy(1, 1)
            xt_copy(1, 2)
            wh_copy(1)
            wh_copy(2)
            act.wait_ge(guard3, 1)
            nc.scalar.activation(V3[:, :], WH[:, :, D + 1], ACT.Exp, bias=C3[:, 0:1]).then_inc(v3_exp, 1)
            nc.scalar.activation(S3[:, :], WH[:, :, D + 1], ACT.Exp, bias=C3[:, 1:2], scale=-0.8)
            for n, (c, w) in enumerate(CHUNKS):
                act.wait_ge(f_mm, n + 1)
                nc.scalar.activation(R3[:, c:c + w], ACC[:, c:c + w], ACT.Exp, bias=C3[:, 1:2], scale=0.8).then_inc(r3_exp, 1)
            for n, (c, w) in enumerate(CHUNKS):
                lo, hi = GROUPS[n]
                act.wait_ge(acc3_mm, n + 1)
                nc.scalar.activation(NUMT[:, c:c + w], ZP[0:W2, c:c + w], ACT.Copy).then_inc(acc3_sb, 1)
                act.wait_ge(elu_in, n + 1)
                nc.scalar.activation(SQ[:, lo:hi, :], CEN[:, lo:hi, :], ACT.Exp).then_inc(elu_exp, 1)

        @block.vector
        def _(dve):
            done = [0]
            chain = sem("dve_chain")

            def link(ins):
                done[0] += 1
                ins.then_inc(chain, 1)
                dve.wait_ge(chain, done[0])

            def wide(ap, n):
                return ap.unsqueeze(2).to_broadcast([P, n, D])

            def thirds(src, dst, lo, hi):
                link(nc.vector.tensor_copy(dst[:, lo:hi, 0:D], src[:, lo:hi, :]))
                link(nc.vector.tensor_tensor(RES[:, lo:hi, :], src[:, lo:hi, :], dst[:, lo:hi, 0:D], ALU.subtract))
                link(nc.vector.tensor_copy(dst[:, lo:hi, D:2 * D], RES[:, lo:hi, :]))
                return nc.vector.tensor_tensor(dst[:, lo:hi, 2 * D:3 * D], RES[:, lo:hi, :], dst[:, lo:hi, D:2 * D], ALU.subtract)

            def tick(ins):
                done[0] += 1
                ins.then_inc(chain, 1)
                return done[0]

            norms = [0]

            def row_sum(src, stat, lo, hi):
                return nc.vector.tensor_reduce(STAT[:, stat, lo:hi], src[:, lo:hi, :], X_AXIS, ALU.add)

            def centre(src, lo, hi):
                return nc.vector.scalar_tensor_tensor(CEN[:, lo:hi, :], wide(STAT[:, 0, lo:hi], hi - lo), -1.0 / D,
                                                      src[:, lo:hi, :], ALU.mult, ALU.add)

            def square(lo, hi):
                return nc.vector.tensor_tensor(SQ[:, lo:hi, :], CEN[:, lo:hi, :], CEN[:, lo:hi, :], ALU.mult)

            def variance(lo, hi):
                return nc.vector.tensor_scalar(STAT[:, 2, lo:hi], STAT[:, 4, lo:hi], 1.0 / D, EPS, ALU.mult, ALU.add)

            def var_of(src, lo, hi):
                link(row_sum(src, 0, lo, hi))
                link(centre(src, lo, hi))
                link(square(lo, hi))
                link(row_sum(SQ, 4, lo, hi))
                variance(lo, hi).then_inc(var_ready, 1)

            def scaled(dst, lo, hi):
                norms[0] += 1
                dve.wait_ge(rstd_ready, norms[0])
                return nc.vector.tensor_tensor(dst[:, lo:hi, :], CEN[:, lo:hi, :], wide(STAT[:, 3, lo:hi], hi - lo), ALU.mult)

            def sum_thirds(dst, lo, hi):
                parts = PSN[:, lo:hi, 0:3 * D].rearrange("p t (s d) -> p t d s", s=3)
                link(nc.vector.tensor_reduce(dst[:, lo:hi, :], parts, X_AXIS, ALU.add))

            link(nc.vector.memset(STAT[:, 7, :], -0.5))
            nc.vector.memset(NEG3[:, 0:1], -1.0)
            nc.vector.memset(NEG3[:, 1:2], -0.8)
            link(nc.vector.memset(NUMT[:, :], 1.0))

            dve.wait_ge(x_in, 32)
            thirds(X[0], XS[0], 0, T).then_inc(xs_ready, 1)
            dve.wait_ge(x0t_sb, 1)
            nc.vector.tensor_scalar(X1R[:, :], ONES[0:D, :], XT[0:D, 1:2], None, ALU.mult).then_inc(x1_rows, 1)
            def hidden_read():
                dve.wait_ge(hid_mm, 1)
                link(nc.vector.tensor_copy(NEIGH[:, :], PS[:, 5, 0:D]))
                own = PSflat[:, 3 * 512:3 * 512 + T * D].rearrange("p (t d) -> p t d", d=D)
                nc.vector.tensor_tensor(CEN[:, :, :], own, NEIGH[:, :].unsqueeze(1).to_broadcast([P, T, D]),
                                        ALU.add).then_inc(hid_read, 1)
                dve.wait_ge(hid_read, 1)

            def scores_begun():
                link(nc.vector.scalar_tensor_tensor(SQ[:, :, :], CEN[:, :, :], 0.01, CEN[:, :, :], ALU.mult, ALU.max))
                dve.wait_ge(atw_in, 32)
                link(nc.vector.tensor_tensor(CEN[:, :, :], SQ[:, :, :], ATW[:, :].unsqueeze(1).to_broadcast([P, T, D]), ALU.mult))

            def scores_ended():
                link(nc.vector.tensor_reduce(SC[:, 1, :], CEN[:, :, :], X_AXIS, ALU.add))
                link(nc.vector.tensor_scalar(SC[:, 0, :], SC[:, 1, :], ATB[:, 0:1], None, ALU.add))
                link(nc.vector.tensor_tensor(SC[:, 1, :], SC[:, 0, :], SC[:, 0, :], ALU.max))
                nc.vector.tensor_tensor(SC[:, 2, :], SC[:, 0, :], SC[:, 1, :], ALU.subtract).then_inc(score_dif, 1)

            def sums0(lo, hi):
                n = hi - lo
                dve.wait_ge(sum0_mm, hi)
                sum_thirds(NRM, lo, hi)
                link(nc.vector.tensor_tensor(RDEN[:, lo:hi], PSN[:, lo:hi, W0 - 1], WROW[:, lo:hi], ALU.mult))
                link(nc.vector.reciprocal(STAT[:, 5, lo:hi], RDEN[:, lo:hi]))
                link(nc.vector.tensor_tensor(STAT[:, 6, lo:hi], STAT[:, 5, lo:hi], WROW[:, lo:hi], ALU.mult))
                link(nc.vector.tensor_tensor(NRM[:, lo:hi, :], NRM[:, lo:hi, :], wide(STAT[:, 6, lo:hi], n), ALU.mult))
                link(nc.vector.tensor_tensor(Y[:, lo:hi, :], NRM[:, lo:hi, :], X[0][:, lo:hi, :], ALU.add))

            def input1(lo, hi):
                link(scaled(X[1], lo, hi))
                thirds(X[1], XS[1], lo, hi).then_inc(x_ready, 1)

            for t in range(T):
                dve.wait_ge(at_mm, t + 1)
                nc.vector.tensor_copy(AT[:, 0:8, t * P:(t + 1) * P], AT_LO).then_inc(at_lo, 1)
                if t == 0:
                    hidden_read()
                    scores_begun()
                if t == 1:
                    scores_ended()
                for g in GROUPS[:-1]:
                    if t == g[1]:
                        dve.wait_ge(score_exp, 1)
                        sums0(*g)
                    if t == g[1] + 1:
                        var_of(Y, *g)
                    if t == g[1] + 2:
                        input1(*g)
            last = GROUPS[-1]
            sums0(*last)
            var_of(Y, *last)
            input1(*last)

            def sums1(lo, hi):
                dve.wait_ge(sum1_mm, hi)
                sum_thirds(NRM, lo, hi)
                link(nc.vector.scalar_tensor_tensor(Y[:, lo:hi, :], X[1][:, lo:hi, :], 2.0, NRM[:, lo:hi, :], ALU.mult, ALU.add))

            def ab_thirds(n):
                c, w = CHUNKS[n]
                dve.wait_ge(hi_ready, n + 1)
                nc.vector.tensor_tensor(R1[:, c:c + w], AB[:, c:c + w], TERMS[0:32, c:c + w], ALU.subtract).then_inc(r1_ready, 1)
                dve.wait_ge(r1_ready, n + 1)
                link(nc.vector.tensor_copy(MID[:, c:c + w], R1[:, c:c + w]))
                nc.vector.tensor_tensor(TERMS[64:96, c:c + w], R1[:, c:c + w], MID[:, c:c + w], ALU.subtract).then_inc(lo_ready, 1)

            written = {}

            def norm_step(k, n, dst):
                lo, hi = GROUPS[n]
                if k < 5:
                    dve.wait_ge(chain, written[n])
                if k == 0:
                    written[n] = tick(row_sum(Y, 0, lo, hi))
                elif k == 1:
                    written[n] = tick(centre(Y, lo, hi))
                elif k == 2:
                    written[n] = tick(square(lo, hi))
                elif k == 3:
                    written[n] = tick(row_sum(SQ, 4, lo, hi))
                elif k == 4:
                    variance(lo, hi).then_inc(var_ready, 1)
                elif k == NORM_STEPS - 1:
                    scaled(dst, lo, hi).then_inc(x_ready, 1)

            def layer1_step(k, n):
                lo, hi = GROUPS[n]
                if k == 0:
                    dve.wait_ge(sum1_mm, hi)
                    parts = PSN[:, lo:hi, 0:3 * D].rearrange("p t (s d) -> p t d s", s=3)
                    written[n] = tick(nc.vector.tensor_reduce(NRM[:, lo:hi, :], parts, X_AXIS, ALU.add))
                elif k == 1:
                    dve.wait_ge(chain, written[n])
                    written[n] = tick(nc.vector.scalar_tensor_tensor(Y[:, lo:hi, :], X[1][:, lo:hi, :], 2.0, NRM[:, lo:hi, :], ALU.mult, ALU.add))
                else:
                    norm_step(k - 2, n, X[2])

            sums1(*GROUPS[0])
            var_of(Y, *GROUPS[0])
            scaled(X[2], *GROUPS[0]).then_inc(x_ready, 1)
            for k in range(2 + NORM_STEPS + SKEW1):
                for n, step in ((1, k), (2, k - SKEW1)):
                    if 0 <= step < 2 + NORM_STEPS:
                        layer1_step(step, n)
            for n in range(len(CHUNKS)):
                ab_thirds(n)

            dve.wait_ge(b0_mm, 1)
            nc.vector.tensor_copy(B0[:, :, :], PS[:, 3, 0:T * H].rearrange("p (t h) -> p t h", h=H)).then_inc(b0_sb, 1)
            dve.wait_ge(at_hi, T)
            link(nc.vector.tensor_reduce(MX[:, 0:1], AB, X_AXIS, ALU.max))
            nc.vector.tensor_scalar(MXR[:, :], ONES[0:4 * H, :], MX[:, 0:1], None, ALU.mult).then_inc(mxr_ready, 1)
            dve.wait_ge(fold_sb, 1)
            nc.vector.tensor_scalar(FREP[:, :], ONES[0:D, :], WA3[:, 0:1], None, ALU.mult).then_inc(f_rows, 1)

            def pick(h, t):
                dve.wait_ge(z0_ready, h * T + t + 1)
                dve.wait_ge(z1_mm, h * T + t + 1)
                dve.sem_inc(tiles_picked, 1)
                nc.vector.copy_predicated(Z[:, t, :], AT[:, t, 0:N].bitcast(U16), ZP).then_inc(z_ready, 1)

            def leaky(h, t):
                dve.wait_ge(z_ready, h * T + t + 1)
                nc.vector.scalar_tensor_tensor(Z[:, t, :], Z[:, t, :], 0.2, Z[:, t, :], ALU.mult, ALU.max).then_inc(leaky_ready, 1)

            def inverted(h):
                dve.wait_ge(back_sb, h + 1)
                dve.wait_ge(num_added, h + 1)
                nc.vector.reciprocal(RDEN[:, :], BACK[:, :, D]).then_inc(rden_ready, 1)

            def guards_found():
                dve.wait_ge(max_mm, 1)
                link(nc.vector.tensor_copy(G2[:, 0, :], PS[:, 0, 0:2 * H]))
                link(nc.vector.tensor_tensor(G2[:, 1, :], PS[:, 0, 2 * H:4 * H], G2[:, 0, :], ALU.add))
                link(nc.vector.scalar_tensor_tensor(G2[:, 2, :], G2[:, 1, :], 0.2, G2[:, 1, :], ALU.mult, ALU.max))
                link(nc.vector.tensor_tensor(G2[:, 0, 0:H], G2[:, 2, 0:H], G2[:, 2, H:2 * H], ALU.max))
                nc.vector.tensor_scalar(NEGC[:, :], G2[:, 0, 0:H], -1.0, None, ALU.mult).then_inc(guards, 1)

            def head(h, first):
                for t in range(T):
                    pick(h, t)
                    if first and t == 0:
                        guards_found()
                    if t > 0:
                        leaky(h, t - 1)
                    elif not first:
                        leaky(h - 1, T - 1)
                    if t == 7 and not first:
                        inverted(h - 1)

            head(0, True)
            with dve.Fori(1, H) as h:
                head(h, False)
            leaky(H - 1, T - 1)

            def output_step(k, n):
                lo, hi = GROUPS[n]
                sums = group_bank(3, n, W2)
                if k == 0:
                    dve.wait_ge(last_mm, n + 1)
                    ins = nc.vector.reciprocal(RDEN[:, lo:hi], sums[:, :, D])
                elif k < 3:
                    dve.wait_ge(chain, written[n])
                if k == 1:
                    ins = nc.vector.tensor_tensor(NRM[:, lo:hi, :], sums[:, :, 0:D], wide(RDEN[:, lo:hi], hi - lo), ALU.mult)
                elif k == 2:
                    ins = nc.vector.tensor_tensor(Y[:, lo:hi, :], Y[:, lo:hi, :], NRM[:, lo:hi, :], ALU.add)
                if k < 3:
                    written[n] = tick(ins)
                else:
                    norm_step(k - 3, n, X[3])

            dve.wait_ge(num_added, H)
            for k in range(3 + NORM_STEPS + SKEW[-1]):
                for n in range(len(GROUPS)):
                    if 0 <= k - SKEW[n] < 3 + NORM_STEPS:
                        output_step(k - SKEW[n], n)

            dve.wait_ge(wh_sb, len(GROUPS))
            nc.vector.tensor_reduce(MX3[:, 0:2], WH[:, 0:T - 1, D + 1:D + 3].rearrange("p t n -> p n t"), X_AXIS, ALU.max)
            link(nc.vector.tensor_reduce(MX3[:, 2:3], WH[:, 0:T - 1, D + 1], X_AXIS, ALU.min))
            nc.vector.tensor_tensor(MX3[0:LAST, 0:2], MX3[0:LAST, 0:2], WH[0:LAST, T - 1, D + 1:D + 3], ALU.max)
            link(nc.vector.tensor_tensor(MX3[0:LAST, 2:3], MX3[0:LAST, 2:3], WH[0:LAST, T - 1, D + 1:D + 2], ALU.min))
            nc.vector.scalar_tensor_tensor(MX3[:, 1:2], MX3[:, 2:3], -1.0, MX3[:, 1:2], ALU.mult, ALU.max).then_inc(max3_ready, 1)
            dve.wait_ge(max3_mm, 1)
            link(nc.vector.tensor_reduce(MX3T[:, P:P + 1], PS[0:2, 6, 0:P], X_AXIS, ALU.max))
            nc.vector.tensor_scalar(MX3T[:, 0:P], ONES[0:2, :], MX3T[:, P:P + 1], None, ALU.mult).then_inc(max3_ready, 1)
            dve.wait_ge(max3_mm, 2)
            nc.vector.tensor_tensor(C3[:, :], PS[:, 6, 0:2], NEG3[:, :], ALU.mult).then_inc(guard3, 1)
            dve.wait_ge(v3_exp, 1)
            link(nc.vector.tensor_tensor(WH[:, :, 0:W2], WH[:, :, 0:W2], V3[:, :].unsqueeze(2).to_broadcast([P, T, W2]), ALU.mult))
            for n, (c, w) in enumerate(CHUNKS):
                dve.wait_ge(r3_exp, n + 1)
                for t in range(T):
                    nc.vector.scalar_tensor_tensor(Z[:, t, c:c + w], R3[:, c:c + w], S3[:, t:t + 1], AT[:, t, c:c + w],
                                                   ALU.max, ALU.mult).then_inc(p3_ready, 1)

            for n, (lo, hi) in enumerate(GROUPS):
                sums = group_bank(0, n, W2)
                dve.wait_ge(num3_mm, n + 1)
                link(nc.vector.reciprocal(RDEN[:, lo:hi], sums[:, :, D]))
                link(nc.vector.tensor_tensor(NRM[:, lo:hi, :], sums[:, :, 0:D], wide(RDEN[:, lo:hi], hi - lo), ALU.mult))
                nc.vector.tensor_scalar(CEN[:, lo:hi, :], NRM[:, lo:hi, :], 0.0, None, ALU.min).then_inc(elu_in, 1)
                link(nc.vector.scalar_tensor_tensor(RES[:, lo:hi, :], NRM[:, lo:hi, :], 0.0, X[3][:, lo:hi, :], ALU.max, ALU.add))
                dve.wait_ge(elu_exp, n + 1)
                link(nc.vector.scalar_tensor_tensor(NRM[:, lo:hi, :], SQ[:, lo:hi, :], -1.0, RES[:, lo:hi, :], ALU.add, ALU.add))
                var_of(NRM, lo, hi)
                scaled(Y, lo, hi).then_inc(x_ready, 1)

        @block.tensor
        def _(pe):
            mm, tr = nc.tensor.matmul, nc.tensor.transpose

            pe.wait_ge(idents, 3)
            pe.wait_ge(x_in, 32)
            for t in range(T):
                ins = tr(PSflat[0:D, t * P:(t + 1) * P], X[0][:, t, :], IDF[:, :])
            ins.then_inc(x0t_mm, 1)
            pe.wait_ge(x0t_sb, 1)
            pe.wait_ge(wb_in, 3 * 16)
            pe.wait_ge(consts, 1)

            def hidden(lo, hi):
                for t in range(lo, hi):
                    mm(PSflat[:, 3 * 512 + t * D:3 * 512 + (t + 1) * D], XT[:, t * P:(t + 1) * P], FC1[:, :], start=True, stop=True)

            hidden(0, 5)

            def adj_transposed(it):
                pe.wait_ge(an_ready, it + 1)
                for j in range(T):
                    ins = tr(PSTR[:, j * P:(j + 1) * P], AN[:, bass.ds(it, 1), j * P:(j + 1) * P].rearrange("p a j -> p (a j)"), IDB[:, :])
                ins.then_inc(at_mm, 1)

            def sums(it, width, signal):
                xs = XS[0] if width == W0 else XS[1]
                for j in range(T):
                    ins = mm(PSN[:, bass.ds(it, 1), 0:width].rearrange("p a n -> p (a n)"),
                             AT[:, j, bass.ds(it * P, P)], xs[:, j, 0:width], start=j == 0, stop=j == T - 1)
                ins.then_inc(signal, 1)

            adj_transposed(0)
            hidden(5, T)
            pe.wait_ge(x1_rows, 1)
            mm(PS[:, 5, 0:D], X1R[:, :], FC2[:, :], start=True, stop=True).then_inc(hid_mm, 1)
            pe.wait_ge(xs_ready, 1)
            pe.wait_ge(consts, 2)
            with pe.Fori(0, (T - 1) // STEPS) as part:
                for it in [STEPS * part + u + 1 for u in range(STEPS)]:
                    pe.wait_ge(at_lo, it)
                    pe.wait_ge(at_hi, it)
                    adj_transposed(it)
                    pe.wait_ge(hid_read, 1)
                    sums(it - 1, W0, sum0_mm)
            pe.wait_ge(at_lo, T)
            pe.wait_ge(at_hi, T)
            sums(T - 1, W0, sum0_mm)

            pe.wait_ge(w_in, 12 * 16)
            pe.wait_ge(x_ready, 2)
            for c in range(4):
                tr(PS[:, 6, c * W2:(c + 1) * W2], QS[:, c * P:(c + 1) * P], IDF[0:W2, 0:W2])
                tr(PS[:, 7, c * W2:(c + 1) * W2], KS[:, c * P:(c + 1) * P], IDF[0:W2, 0:W2])
            for h in range(H):
                tr(PS[0:D, h // 4, h % 4 * W2:(h % 4 + 1) * W2], VS[:, h * D:(h + 1) * D], IDF[0:W2, 0:W2])
            tr(PS[0:D, 2, 0:D], W3S[0:D, 0:D], IDF[0:D, 0:D]).then_inc(wts_mm, 1)
            pe.wait_ge(wts_sb, 1)
            for half in range(2):
                for c in range(4):
                    mm(PS[0:W2, 3, half * 2 * H:(half + 1) * 2 * H], QKT[:, 4 * half + c, :],
                       AW[:, 4 * half + c, :, :].rearrange("p k h -> p (k h)"), start=c == 0, stop=c == 3)
            mm(PS[0:D, 3, 64:66], WT[:, :], A3[:, :], start=True, stop=True)
            for h in range(H):
                ins = mm(PS[0:W2, 6, h * D:(h + 1) * D], VWT[:, h, :], PWS[:, h, :], start=True, stop=True)
            ins.then_inc(fold_mm, 1)

            pe.wait_ge(x_ready, len(GROUPS))
            with pe.Fori(0, 2) as group:
                for u in range(4):
                    if u == 2:
                        pe.wait_ge(fold_sb, 1)
                    sums(4 * group + u, 3 * D, sum1_mm)

            def x_transposed(layer, src, n):
                lo, hi = GROUPS[n]
                pe.wait_ge(x_ready, len(GROUPS) * (layer + 1) + n + 1)
                if n == 2:
                    pe.wait_ge(xt_sb, len(GROUPS) * layer + 1)
                for t in range(lo, hi):
                    ins = tr(PS[0:D, 6 + n % 2, (t - lo) * P:(t - lo + 1) * P], src[:, t, :], IDF[:, :])
                ins.then_inc(xt_mm, 1)

            def ab(n):
                c, w = CHUNKS[n]
                pe.wait_ge(xt_sb, n + 1)
                if n > 0:
                    pe.wait_ge(hi_ready, n)
                mm(PS[0:4 * H, 0, 0:w], W32[:, :], XT[:, c:c + w], start=True, stop=True).then_inc(ab_mm, 1)

            def b0(lo, hi):
                for t in range(lo, hi):
                    ins = mm(PS[:, 3, t * H:(t + 1) * H], XT[:, t * P:(t + 1) * P], W32[:, 2 * H:3 * H], start=True, stop=True)
                return ins

            def values(lo, hi):
                for t in range(lo, hi):
                    if t >= 3:
                        pe.wait_ge(vall_sb, t - 1)
                    mm(PS[:, vall_bank(t), :], XT[:, t * P:(t + 1) * P], VP[:, :], start=True, stop=True).then_inc(val_mm, 1)

            def row_of_first(half):
                dst = MISC if half == 0 else PSflat[:, 512:]
                for c in range(0, HALF, 512):
                    w = min(512, HALF - c)
                    ins = mm(dst[:, c:c + w], PICK0[:, :], TERMS[:, half * HALF + c:half * HALF + c + w], start=True, stop=True)
                ins.then_inc(row_mm, 1)

            sums(8, 3 * D, sum1_mm)
            sums(9, 3 * D, sum1_mm)
            x_transposed(0, X[2], 0)
            sums(10, 3 * D, sum1_mm)
            ab(0)
            values(0, 1)
            x_transposed(0, X[2], 1)
            ab(1)
            x_transposed(0, X[2], 2)
            b0(0, 8)
            ab(2)
            b0(8, T).then_inc(b0_mm, 1)
            pe.wait_ge(mid_ready, 2)
            pe.wait_ge(lo_ready, 2)
            row_of_first(0)

            def z1(h, t):
                for c, w in CHUNKS:
                    ins = mm(ZP[:, c:c + w], LHS1[:, bass.ds(h, 1), t * P:(t + 1) * P].rearrange("p a n -> p (a n)"),
                             TERMS[:, c:c + w], start=True, stop=True)
                ins.then_inc(z1_mm, 1)

            def weigh(h, t, par, first):
                k = rows_of(t)
                if first:
                    pe.wait_ge(v0_set, t + 1)
                elif t == 0:
                    pe.wait_ge(val_sb, h)
                pe.wait_ge(p_ready, h * T + t + 1)
                for n, (c, w) in enumerate(CHUNKS):
                    if t == 0 and not first:
                        pe.wait_ge(acc_sb, 3 * (h - 1) + n + 1)
                    ins = mm(ACC[0:W2, c:c + w], VST[par][0:k, t, :], Z[0:k, t, c:c + w], start=t == 0, stop=t == T - 1)
                    if t == T - 1:
                        ins.then_inc(acc_mm, 1)
                    if n == len(CHUNKS) - 1 and t < T - 1:
                        ins.then_inc(p_used, 1)
                if t == T - 1:
                    pe.sem_inc(p_used, 1)

            def sums_back(h):
                pe.wait_ge(acc_sb, 3 * h + 3)
                for t in range(T):
                    ins = tr(v_block(t), NUMT[:, t * P:(t + 1) * P], IDF[0:W2, 0:W2])
                ins.then_inc(num_mm, 1)

            def head(h, par, first, last):
                for t in range(T):
                    pe.wait_ge(z_ready, h * T + t + 1)
                    if first and (t + 1) * P == B1_FIRST:
                        pe.wait_ge(b1_in[1], 3 * 16)
                    if t < T - 1:
                        z1(h, t + 1)
                    elif not last:
                        z1(h + 1, 0)
                    if t >= 3:
                        weigh(h, t - 3, par, first)
                    elif not first:
                        weigh(h - 1, T - 3 + t, 1 - par, False)
                    if first and t < T - 3:
                        values(t + 3, t + 4)
                    if t == 4 and not first:
                        sums_back(h - 1)

            pe.wait_ge(mid_ready, len(CHUNKS))
            pe.wait_ge(lo_ready, len(CHUNKS))
            pe.wait_ge(vall_sb, 1)
            row_of_first(1)
            pe.wait_ge(b0_sb, 1)
            pe.wait_ge(b1_in[0], 3 * 16)
            z1(0, 0)
            pe.wait_ge(row_sb, 1)
            values(1, 2)
            pe.wait_ge(mxr_ready, 1)
            mm(PS[:, 0, 0:4 * H], MXR[:, :], IDF[0:4 * H, 0:4 * H], start=True, stop=True).then_inc(max_mm, 1)
            values(2, 3)
            pe.wait_ge(row_sb, 2)
            head(0, 0, True, False)
            pe.wait_ge(v0_set, T)
            with pe.Fori(0, H // 2 - 1) as pair:
                head(2 * pair + 1, 1, False, False)
                head(2 * pair + 2, 0, False, False)
            head(H - 1, 1, False, True)

            def weigh_last(n, lo, hi):
                c, w = CHUNKS[n]
                for t in range(lo, hi):
                    k = rows_of(t)
                    pe.wait_ge(p_ready, (H - 1) * T + t + 1)
                    ins = mm(ACC[0:W2, c:c + w], VST[1][0:k, t, :], Z[0:k, t, c:c + w], start=False, stop=t == T - 1)
                if hi == T:
                    ins.then_inc(acc_mm, 1)

            def last_back(n):
                lo, hi = GROUPS[n]
                pe.wait_ge(acc_sb, 3 * (H - 1) + n + 1)
                for t in range(lo, hi):
                    ins = tr(PS[:, 3 + n, (t - lo) * W2:(t - lo + 1) * W2], NUMT[:, t * P:(t + 1) * P], IDF[0:W2, 0:W2])
                ins.then_inc(last_mm, 1)

            weigh_last(0, T - 3, T)
            weigh_last(1, T - 3, T - 2)
            last_back(0)
            weigh_last(1, T - 2, T)
            weigh_last(2, T - 3, T - 1)
            last_back(1)
            weigh_last(2, T - 1, T)
            last_back(2)

            def features3(n):
                lo, hi = GROUPS[n]
                pe.wait_ge(xt_sb, len(GROUPS) + n + 1)
                for t in range(lo, hi):
                    ins = mm(PS[:, 3 + n, (t - lo) * W3:(t - lo + 1) * W3], XT[:, t * P:(t + 1) * P], W3S[:, :], start=True, stop=True)
                ins.then_inc(wh_mm, 1)

            def f_row(lo, hi):
                return mm(ACC[:, lo:hi], FREP[:, :], XT[0:D, lo:hi], start=True, stop=True)

            def weigh3(n, lo, hi):
                c, w = CHUNKS[n]
                for t in range(lo, hi):
                    k = rows_of(t)
                    pe.wait_ge(p3_ready, n * T + t + 1)
                    ins = mm(ZP[0:W2, c:c + w], WH[0:k, t, 0:W2], Z[0:k, t, c:c + w], start=t == 0, stop=t == T - 1)
                if hi == T:
                    ins.then_inc(acc3_mm, 1)

            x_transposed(1, X[3], 0)
            features3(0)
            x_transposed(1, X[3], 1)
            x_transposed(1, X[3], 2)
            features3(1)
            features3(2)
            pe.wait_ge(wh_sb, len(GROUPS))
            pe.wait_ge(max3_ready, 1)
            tr(PS[0:2, 6, 0:P], MX3[:, 0:2], IDF[:, :]).then_inc(max3_mm, 1)
            pe.wait_ge(f_rows, 1)
            f_row(0, 256)
            pe.wait_ge(max3_ready, 2)
            mm(PS[:, 6, 0:2], MX3T[:, 0:P], IDF[0:2, 0:2], start=True, stop=True).then_inc(max3_mm, 1)
            f_row(256, 512).then_inc(f_mm, 1)
            for c, w in CHUNKS[1:]:
                f_row(c, c + w).then_inc(f_mm, 1)

            def group3_back(n):
                lo, hi = GROUPS[n]
                pe.wait_ge(acc3_sb, n + 1)
                pe.wait_ge(r3_exp, len(CHUNKS))
                for t in range(lo, hi):
                    ins = tr(PS[:, n, (t - lo) * W2:(t - lo + 1) * W2], NUMT[:, t * P:(t + 1) * P], IDF[0:W2, 0:W2])
                ins.then_inc(num3_mm, 1)

            weigh3(0, 0, T)
            weigh3(1, 0, 3)
            group3_back(0)
            weigh3(1, 3, T)
            weigh3(2, 0, 3)
            group3_back(1)
            weigh3(2, 3, T)
            group3_back(2)


_INS = ['x', 'adj', 'L0_gnn_fc_w', 'L0_gnn_fc_b', 'L0_gnn_attn_w', 'L0_gnn_attn_b', 'L2_gnn_Qw', 'L2_gnn_Qb',
        'L2_gnn_Kw', 'L2_gnn_Kb', 'L2_gnn_Vw', 'L2_gnn_Vb', 'L2_gnn_a', 'L2_gnn_Pw', 'L2_gnn_Pb', 'L3_gnn_W', 'L3_gnn_a']


def kernel(**inputs):
    import concourse.bacc as _bacc
    from concourse.bass_utils import run_bass_kernel_spmd as _run

    nc = _bacc.Bacc("TRN2", target_bir_lowering=False, num_devices=1)
    arrays, args = {}, []
    for name in _INS:
        arr = np.ascontiguousarray(inputs[name])
        arrays[f"in_{name}_dram"] = arr
        args.append(nc.dram_tensor(f"in_{name}_dram", arr.shape, mybir.dt.from_np(arr.dtype), kind="ExternalInput").ap())
    args.append(nc.dram_tensor("out_dram", (N, D), F32, kind="ExternalOutput").ap())
    args.append(nc.dram_tensor("a0_rows_dram", (H, N), F32, kind="Internal").ap())
    graph_kernel(nc, *args)
    r = _run(nc, [arrays], core_ids=[0])
    return r.results[0]["out_dram"]
```
